# Optimizing a Trainium2 kernel written in Bass

```python
import numpy as np
import jax
import jax.numpy as jnp

def _softmax(x, axis=-1):
    return jax.nn.softmax(x, axis=axis)

def _gelu(x):
    return jax.nn.gelu(x, approximate=True)

def _silu(x):
    return jax.nn.silu(x)

def _sigmoid(x):
    return jax.nn.sigmoid(x)

def _layernorm(x, axis=-1, eps=1e-05):
    m = jnp.mean(x, axis=axis, keepdims=True)
    v = jnp.var(x, axis=axis, keepdims=True)
    return (x - m) / jnp.sqrt(v + eps)

def _scatter_add(tgt, idx, src, axis=0):
    return tgt.at[idx].add(src)

def _segment_sum(src, seg, n):
    return jax.ops.segment_sum(src, seg, n)
kernel_name = 'mk_cond_resid_d4_seqx_r4_70487d'

def setup_inputs(seed: int=0):
    np.random.seed(seed)
    _w = jnp.asarray

    def _rec_inputs():
        import jax
        import jax.numpy as jnp
        _rk = jax.random.key(seed)
        x = -0.000125 + 0.9999 * jax.random.normal(jax.random.fold_in(_rk, 1), (8, 256, 1024), jnp.float32)
        _lenS = 256 - jax.random.randint(jax.random.fold_in(_rk, 7), (8,), 0, max(1, 256 // 4) + 1, jnp.int32)
        _lenS2 = 256 - jax.random.randint(jax.random.fold_in(_rk, 8), (8,), 0, max(1, 256 // 4) + 1, jnp.int32)
        itok_B_0_23 = jax.random.randint(jax.random.fold_in(_rk, 11), (8,), 0, 24, jnp.int32)
        itok_B_2_6 = jax.random.randint(jax.random.fold_in(_rk, 12), (8,), 2, 7, jnp.int32)
        itok_B_4_50 = jax.random.randint(jax.random.fold_in(_rk, 13), (8,), 4, 51, jnp.int32)
        itok_B_3_7 = jax.random.randint(jax.random.fold_in(_rk, 14), (8,), 3, 8, jnp.int32)
        return (x, itok_B_0_23, itok_B_2_6, itok_B_4_50, itok_B_3_7)
    x, itok_B_0_23, itok_B_2_6, itok_B_4_50, itok_B_3_7 = _rec_inputs()

    def _L0_cond_setup():
        import jax, jax.numpy as jnp
        import numpy as np
        R = 16
        ALPHA = 32
        SCALING = ALPHA / R
        SLOTS = 32
        IN_F = 1024
        OUT_F = 1024
        B, T = (8, 256)
        key = jax.random.key(seed)
        k1, k2, k3, k4, k5, k6 = jax.random.split(key, 6)
        x = jax.random.normal(k1, (B, T, IN_F), dtype=jnp.float32)
        adapter_mapping = jax.random.randint(k2, (B,), 0, SLOTS, dtype=jnp.int32)
        W = jax.random.normal(k3, (OUT_F, IN_F), dtype=jnp.float32) * 0.02
        b = jax.random.normal(k4, (OUT_F,), dtype=jnp.float32) * 0.02
        lora_As = jax.random.normal(k5, (SLOTS, IN_F, R), dtype=jnp.float32) * 0.02
        lora_Bs = jax.random.normal(k6, (SLOTS, R, OUT_F), dtype=jnp.float32) * 0.02
        return {'x': x, 'adapter_mapping': adapter_mapping, 'W': W, 'b': b, 'lora_As': lora_As, 'lora_Bs': lora_Bs}
    _L0_cond_all = _L0_cond_setup()
    _L0_cond_in = {k: v for k, v in _L0_cond_all.items() if k in ('W', 'b', 'lora_As', 'lora_Bs')}
    del _L0_cond_all

    def _L1_cond_setup():
        import jax, jax.numpy as jnp
        import numpy as np
        B, N, H, F = (4, 128, 1024, 2752)
        L, R, RANK = (1, 16, 16)
        SCALE = 0.5
        key = jax.random.key(seed)
        ks = jax.random.split(key, 12)
        nrm = lambda k, shape, fan: jax.random.normal(k, shape, jnp.float32) * fan ** (-0.5)
        inp = {'x': jax.random.normal(ks[0], (B, N, H), jnp.float32), 'W_gate': nrm(ks[1], (F, H), H), 'W_up': nrm(ks[2], (F, H), H), 'W_down': nrm(ks[3], (H, F), F), 'A_gate': nrm(ks[4], (L, R, RANK, H), H), 'B_gate': nrm(ks[5], (L, R, F, RANK), RANK), 'A_up': nrm(ks[6], (L, R, RANK, H), H), 'B_up': nrm(ks[7], (L, R, F, RANK), RANK), 'A_down': nrm(ks[8], (L, R, RANK, F), F), 'B_down': nrm(ks[9], (L, R, H, RANK), RANK), 'lora_indices': jax.random.randint(ks[10], (B,), 0, R), 'layer_idx': 0}
        return inp
    _L1_cond_all = _L1_cond_setup()
    _L1_cond_in = {k: v for k, v in _L1_cond_all.items() if k in ('W_gate', 'W_up', 'W_down', 'A_gate', 'B_gate', 'A_up', 'B_up', 'A_down', 'B_down')}
    del _L1_cond_all

    def _L2_cond_setup():
        import jax, jax.numpy as jnp
        import numpy as np
        RANK = 16
        ALPHA = 16.0
        SCALING = ALPHA / RANK
        key = jax.random.key(seed)
        k1, k2, k3, k4 = jax.random.split(key, 4)
        batch, n_tok, d_in, d_out, n_adapters, rank = (8, 512, 1024, 1024, 64, RANK)
        x = jax.random.normal(k1, (batch, n_tok, d_in), dtype=jnp.float32)
        A = jax.random.normal(k2, (n_adapters, d_out, rank), dtype=jnp.float32) * 0.02
        B = jax.random.normal(k3, (n_adapters, rank, d_in), dtype=jnp.float32)
        adapter_ids = jax.random.randint(k4, (batch,), 0, n_adapters, dtype=jnp.int32)
        return {'x': x, 'A': A, 'B': B, 'adapter_ids': adapter_ids}
    _L2_cond_all = _L2_cond_setup()
    _L2_cond_in = {k: v for k, v in _L2_cond_all.items() if k in ('A', 'B')}
    del _L2_cond_all

    def _L3_cond_setup():
        import jax, jax.numpy as jnp
        import numpy as np
        RANK = 16
        ALPHA = 16.0
        SCALING = ALPHA / RANK
        N_ADAPTERS = 8
        IN_F = 1024
        OUT_F = 1024
        BATCH = 4
        SEQ = 512
        key = jax.random.key(seed)
        kx, ka, kb, ki = jax.random.split(key, 4)
        x = jax.random.normal(kx, (BATCH, SEQ, IN_F), dtype=jnp.float32)
        A = jax.random.normal(ka, (N_ADAPTERS, OUT_F, RANK), dtype=jnp.float32) * 0.02
        B = jax.random.normal(kb, (N_ADAPTERS, RANK, IN_F), dtype=jnp.float32) * 0.02
        adapter_ids = jax.random.randint(ki, (BATCH,), 0, N_ADAPTERS, dtype=jnp.int32)
        return {'x': x, 'A': A, 'B': B, 'adapter_ids': adapter_ids}
    _L3_cond_all = _L3_cond_setup()
    _L3_cond_in = {k: v for k, v in _L3_cond_all.items() if k in ('A', 'B')}
    del _L3_cond_all
    return {'x': x, 'itok_B_0_23': itok_B_0_23, 'itok_B_2_6': itok_B_2_6, 'itok_B_4_50': itok_B_4_50, 'itok_B_3_7': itok_B_3_7, 'L0_cond_W': _L0_cond_in['W'], 'L0_cond_b': _L0_cond_in['b'], 'L0_cond_lora_As': _L0_cond_in['lora_As'], 'L0_cond_lora_Bs': _L0_cond_in['lora_Bs'], 'L1_cond_W_gate': _L1_cond_in['W_gate'], 'L1_cond_W_up': _L1_cond_in['W_up'], 'L1_cond_W_down': _L1_cond_in['W_down'], 'L1_cond_A_gate': _L1_cond_in['A_gate'], 'L1_cond_B_gate': _L1_cond_in['B_gate'], 'L1_cond_A_up': _L1_cond_in['A_up'], 'L1_cond_B_up': _L1_cond_in['B_up'], 'L1_cond_A_down': _L1_cond_in['A_down'], 'L1_cond_B_down': _L1_cond_in['B_down'], 'L2_cond_A': _L2_cond_in['A'], 'L2_cond_B': _L2_cond_in['B'], 'L3_cond_A': _L3_cond_in['A'], 'L3_cond_B': _L3_cond_in['B']}

def reference(x, itok_B_0_23, itok_B_2_6, itok_B_4_50, itok_B_3_7, L0_cond_W, L0_cond_b, L0_cond_lora_As, L0_cond_lora_Bs, L1_cond_W_gate, L1_cond_W_up, L1_cond_W_down, L1_cond_A_gate, L1_cond_B_gate, L1_cond_A_up, L1_cond_B_up, L1_cond_A_down, L1_cond_B_down, L2_cond_A, L2_cond_B, L3_cond_A, L3_cond_B):
    import jax
    import jax.numpy as jnp

    def _L0_cond_ref(x, adapter_mapping, W, b, lora_As, lora_Bs):
        import jax, jax.numpy as jnp
        import numpy as np
        R = 16
        ALPHA = 32
        SCALING = ALPHA / R
        SLOTS = 32
        IN_F = 1024
        OUT_F = 1024
        B, T = (8, 256)
        base_out = jnp.einsum('bti,oi->bto', x, W) + b
        A = lora_As[adapter_mapping]
        Bm = lora_Bs[adapter_mapping]
        lora_h = jnp.einsum('bti,bir->btr', x, A)
        lora_out = jnp.einsum('btr,bro->bto', lora_h, Bm)
        return base_out + lora_out * SCALING

    def _L1_cond_ref(x, W_gate, W_up, W_down, A_gate, B_gate, A_up, B_up, A_down, B_down, lora_indices, layer_idx):
        import jax, jax.numpy as jnp
        import numpy as np
        B, N, H, F = (4, 128, 1024, 2752)
        L, R, RANK = (1, 16, 16)
        SCALE = 0.5

        def lora_add(base, inp, A, B):
            Ab = A[layer_idx][lora_indices]
            Bb = B[layer_idx][lora_indices]
            t = jnp.einsum('bri,bni->bnr', Ab, inp)
            return base + jnp.einsum('bor,bnr->bno', Bb, t) * SCALE
        gate = lora_add(jnp.einsum('bnh,fh->bnf', x, W_gate), x, A_gate, B_gate)
        up = lora_add(jnp.einsum('bnh,fh->bnf', x, W_up), x, A_up, B_up)
        act = jax.nn.silu(gate) * up
        down = lora_add(jnp.einsum('bnf,hf->bnh', act, W_down), act, A_down, B_down)
        return down

    def _L2_cond_ref(x, A, B, adapter_ids):
        import jax, jax.numpy as jnp
        import numpy as np
        RANK = 16
        ALPHA = 16.0
        SCALING = ALPHA / RANK
        B_req = B[adapter_ids]
        A_req = A[adapter_ids]
        Bx = jnp.einsum('bni,bri->bnr', x, B_req)
        out = jnp.einsum('bnr,bor->bno', Bx, A_req)
        return out * SCALING

    def _L3_cond_ref(x, A, B, adapter_ids):
        import jax, jax.numpy as jnp
        import numpy as np
        RANK = 16
        ALPHA = 16.0
        SCALING = ALPHA / RANK
        N_ADAPTERS = 8
        IN_F = 1024
        OUT_F = 1024
        BATCH = 4
        SEQ = 512
        B_sel = B[adapter_ids]
        A_sel = A[adapter_ids]
        Bx = jnp.einsum('bni,bri->bnr', x, B_sel)
        out = jnp.einsum('bnr,bor->bno', Bx, A_sel)
        return out * SCALING
    x = x + _L0_cond_ref(x, itok_B_0_23, L0_cond_W, L0_cond_b, L0_cond_lora_As, L0_cond_lora_Bs)
    x = x + _L1_cond_ref(x, L1_cond_W_gate, L1_cond_W_up, L1_cond_W_down, L1_cond_A_gate, L1_cond_B_gate, L1_cond_A_up, L1_cond_B_up, L1_cond_A_down, L1_cond_B_down, itok_B_2_6, 0)
    x = x + _L2_cond_ref(x, L2_cond_A, L2_cond_B, itok_B_4_50)
    x = x + _L3_cond_ref(x, L3_cond_A, L3_cond_B, itok_B_3_7)
    return x

_drawn_inputs = setup_inputs


def setup_inputs(seed=0):
    import zlib

    import numpy as np

    out = dict(_drawn_inputs(seed))
    spreads = {}
    factors = {'L0_cond_b': 3.0}
    for name, (base, spread) in spreads.items():
        noise = np.random.default_rng([zlib.crc32(name.encode()), seed]).standard_normal(out[name].shape)
        drawn = base * np.exp(spread * noise) if base else spread * noise
        out[name] = jnp.asarray(drawn.astype(out[name].dtype))
    for name, factor in factors.items():
        out[name] = (out[name] * factor).astype(out[name].dtype)
    return out
```

```python
from contextlib import ExitStack

import numpy as np

import concourse.bass as bass
from concourse import mybir

ALU = mybir.AluOpType
ACT = mybir.ActivationFunctionType
F32 = mybir.dt.float32
F32R = mybir.dt.float32r
I32 = mybir.dt.int32

P = 128
TOKENS, H, F, RANK = 2048, 1024, 2752, 16
BATCH = 256
TB = 512
NTB = TOKENS // TB
NB = TB // BATCH
KH = H // P
FULL = F // P
FT = FULL + 1
TAIL = F - FULL * P
GRP = 4 * RANK
SCALE0, SCALE1 = 2.0, 0.5

I_AX = 0
I_L0 = 1
I_GU = I_L0 + KH
I_UV = I_GU + 2 * FT
I_DN = I_UV + 1
I_S2 = I_DN + 3 * KH
I_S3 = I_S2 + 1
NPIECE = I_S3 + 1
RAWS = 4
assert NPIECE % RAWS == 0 and TAIL * 2 == P

BCOL = KH * P
DCOL = BCOL + P
RAW = DCOL + NB * RANK
SPL = DCOL + P
DN_TILES = (8, 8, 6)

LOADS = [0] * NPIECE
LOADS[I_AX] = 2 * NB
for _m in range(KH):
    LOADS[I_L0 + _m] = 1 + NB
for _f in range(FT):
    LOADS[I_GU + 2 * _f] = 1 + NB
    LOADS[I_GU + 2 * _f + 1] = (1 if _f < FULL else 0) + NB + (NB if _f else 0)
LOADS[I_UV] = 3 * NB
for _m in range(KH):
    LOADS[I_DN + 3 * _m] = LOADS[I_DN + 3 * _m + 1] = 1
    LOADS[I_DN + 3 * _m + 2] = 1 + NB
LOADS[I_S2] = LOADS[I_S3] = NB
SLOT_LOADS = [sum(LOADS[s::RAWS]) for s in range(RAWS)]


def landed(idx):
    return sum(LOADS[idx % RAWS:idx + 1:RAWS])


def wnum(idx):
    return idx - 1 if idx < I_UV else idx - 2


NW = wnum(I_S3) + 1
assert NW % 2 == 0

PC_RAW = NPIECE // RAWS
PC_SPLIT = NW // 2
N_T = 6
N_A = 4 * KH


def adapted_layers(nc, x, bias, idx, w0, wgu, wdn, a0, agu, b0, bg, bu, ad, bd, uf, vf, s2, s3, masks, out):
    with ExitStack() as ctx:
        def sb(name, shape, dt):
            return ctx.enter_context(nc.sbuf_tensor(name, shape, dt))

        def sem(name):
            return ctx.enter_context(nc.semaphore(name))

        xhi = sb("xhi", [P, KH, TB], F32R)
        xlo = sb("xlo", [P, KH, TB], F32R)
        acthi = sb("acthi", [P, FULL, TB], F32R)
        actlo = sb("actlo", [P, FULL, TB], F32R)
        tail = sb("tail", [P, TB], F32R)
        res = sb("res", [P, 2, KH, TB], F32)
        ax0 = sb("ax0", [P, KH, P], F32R)
        axp = sb("axp", [P, 2, KH, P], F32R)
        r0 = sb("r0", [P, TB], F32R)
        r1 = sb("r1", [P, TB], F32R)
        r2 = sb("r2", [P, TB], F32R)
        scratch = sb("scratch", [P, TB], F32)
        whi = sb("whi", [P, 2, SPL], F32R)
        wlo = sb("wlo", [P, 2, BCOL], F32R)
        raw = sb("raw", [P, RAWS, RAW], F32)
        bias_sb = sb("bias_sb", [P, KH], F32)
        mask_sb = sb("mask_sb", [P, 2], F32)
        idx_sb = sb("idx_sb", [1, NTB * 4 * NB], I32)
        acc = [ctx.enter_context(nc.psum_tensor(f"acc{i}", [P, TB], F32)) for i in range(4)]
        tps = [ctx.enter_context(nc.psum_tensor(f"tps{i}", [P, TB], F32)) for i in range(4)]
        t_bank = [tps[0], tps[1], tps[2], tps[3], tps[1], tps[2]]
        t_rows = [r0, r1, r2, r0, r1, r2]
        T0, TG, TU, TD, T2, T3 = range(N_T)

        const_in = sem("const_in")
        zeroed = sem("zeroed")
        x_full = sem("x_full")
        raw_full = [sem(f"raw_full{s}") for s in range(RAWS)]
        hi_done = sem("hi_done")
        split_done = [sem(f"split_done{s}") for s in range(RAWS)]
        ax0_hi = sem("ax0_hi")
        ax0_done = sem("ax0_done")
        slot_done = [sem(f"slot_done{s}") for s in range(2)]
        t_full = sem("t_full")
        h_ready = sem("h_ready")
        r_done = sem("r_done")
        a_hi = sem("a_hi")
        a_done = sem("a_done")
        y_done = sem("y_done")
        silu_done = sem("silu_done")
        prod_done = sem("prod_done")
        act_hi = sem("act_hi")
        act_done = sem("act_done")
        s_acc = sem("s_acc")
        out_done = [sem(f"out_done{p}") for p in range(2)]

        block = ctx.enter_context(nc.Block())

        class At:
            def __init__(self, pair, par):
                self.pair, self.par = pair, par

            def __call__(self, per_block, n):
                return self.pair * (2 * per_block) + (self.par * per_block + n)

        @block.sync
        def _(sp):
            sp.dma_start(idx_sb[:], idx).then_inc(const_in, 16)
            sp.dma_start(bias_sb[:], bias).then_inc(const_in, 16)
            sp.dma_start(mask_sb[:], masks).then_inc(const_in, 16)
            sp.wait_ge(const_in, 48)

            def load_piece(at, idx0, step, per_step, parts):
                s = idx0 % RAWS
                sp.wait_ge(split_done[s], at(PC_RAW, idx0 // RAWS) + step * (per_step // RAWS))
                for dst, src in parts:
                    sp.dma_start(dst(s), src).then_inc(raw_full[s], 16)

            def cols(a, b):
                return lambda s: raw[:, s, a:b]

            def rows(j, a, b):
                return lambda s: raw[GRP * j:GRP * (j + 1), s, a:b]

            def of(array, i):
                return array[bass.ds(i, 1)].rearrange("o p c -> (o p) c")

            def of2(array, i, k):
                return array[bass.ds(i, 1), bass.ds(k, 1)].rearrange("o q p c -> (o q p) c")

            with sp.Fori(0, NTB // 2) as pair:
                for par in range(2):
                    at = At(pair, par)
                    n = 4 * NB
                    base = pair * (2 * n) + par * n
                    e = [[sp.value_load(idx_sb[0:1, bass.ds(base + NB * kind + j, 1)], min_val=0, max_val=top - 1)
                          for j in range(NB)]
                         for kind, top in enumerate((a0.shape[0], agu.shape[0], uf.shape[0], vf.shape[0]))]
                    sp.wait_ge(out_done[par], pair * (16 * KH))
                    sp.dma_start(res[:, par, :, :].rearrange("p k n -> p (k n)"),
                                 x[bass.ds(pair * 2 + par, 1)].rearrange("o p c -> (o p) c")).then_inc(x_full, 16)
                    load_piece(at, I_AX, 0, 0,
                               [(cols(P * j, P * (j + 1)), of(a0, e[0][j])) for j in range(NB)]
                               + [(cols(2 * P * (j + 1), 2 * P * (j + 2)), of(agu, e[1][j])) for j in range(NB)])
                    with sp.Fori(0, KH // RAWS) as i:
                        for m in range(RAWS):
                            load_piece(at, I_L0 + m, i, RAWS,
                                       [(cols(0, BCOL), of(w0, i * RAWS + m))]
                                       + [(rows(j, BCOL, DCOL), of2(b0, e[0][j], i * RAWS + m)) for j in range(NB)])

                    def gate_up(i, f0, kinds):
                        for h, (main, before) in enumerate(kinds):
                            f = i * 2 + (f0 + h)
                            g = i * 4 + 2 * (f0 + h)
                            k = I_GU + 2 * (f0 + h)
                            load_piece(at, k, i, RAWS,
                                       [(cols(0, BCOL), of(wgu, g))]
                                       + [(rows(j, BCOL, DCOL), of2(bg, e[1][j], f)) for j in range(NB)])
                            load_piece(at, k + 1, i, RAWS,
                                       ([(cols(0, BCOL), of(wgu, g + 1))] if main else [])
                                       + [(rows(j, BCOL, DCOL), of2(bu, e[1][j], f)) for j in range(NB)]
                                       + ([(cols(DCOL + RANK * j, DCOL + RANK * (j + 1)), of2(ad, e[1][j], f - 1))
                                           for j in range(NB)] if before else []))

                    gate_up(0, 0, [(True, False), (True, True)])
                    with sp.Fori(0, (FT - 4) // 2) as i:
                        gate_up(i, 2, [(True, True), (True, True)])
                    gate_up(0, FT - 2, [(True, True), (False, True)])
                    load_piece(at, I_UV, 0, 0,
                               [(cols(2 * P * j, 2 * P * j + P), of(uf, e[2][j])) for j in range(NB)]
                               + [(cols(2 * P * j + P, 2 * P * j + 2 * P), of(vf, e[3][j])) for j in range(NB)]
                               + [(cols(DCOL + RANK * j, DCOL + RANK * (j + 1)),
                                   ad[bass.ds(e[1][j], 1), FT - 1].rearrange("o p c -> (o p) c")) for j in range(NB)])
                    with sp.Fori(0, 2) as i:
                        for m in range(4):
                            for q, c0 in enumerate((0, 8, 16)):
                                w = DN_TILES[q] * P
                                load_piece(at, I_DN + 3 * m + q, i, 3 * 4,
                                           [(cols(0, w), of(wdn, i * 4 + m)[:, c0 * P:c0 * P + w])]
                                           + ([(rows(j, w, w + P), of2(bd, e[1][j], i * 4 + m)) for j in range(NB)]
                                              if q == 2 else []))
                    load_piece(at, I_S2, 0, 0, [(rows(j, 0, BCOL), of(s2, e[2][j])) for j in range(NB)])
                    load_piece(at, I_S3, 0, 0, [(rows(j, 0, BCOL), of(s3, e[3][j])) for j in range(NB)])

        @block.gpsimd
        def _(pool):
            with pool.Fori(0, NTB // 2) as pair:
                for par in range(2):
                    at = At(pair, par)
                    for m in range(KH):
                        pool.wait_ge(y_done, at(N_A, 3 * KH + m + 1))
                        pool.dma_start(out[bass.ds(pair * 2 + par, 1), m].rearrange("o p c -> (o p) c"),
                                       res[:, par, m, :]).then_inc(out_done[par], 16)
            for par in range(2):
                pool.wait_ge(out_done[par], 16 * KH * (NTB // 2))

        @block.scalar
        def _(act):
            def rounded(dst, src, scale=1.0):
                return nc.scalar.activation(dst, src, ACT.Copy, scale=scale)

            def factor_hi(dst, src, scale):
                n = src.shape[1]
                return rounded(dst[:, :, 0:3 * RANK].rearrange("p n (g r) -> p n g r", g=3),
                               src.unsqueeze(2).to_broadcast([P, n, 3, RANK]), scale)

            def wait_raw(at, idx, i=0, per_step=0):
                s = idx % RAWS
                step = landed(idx + per_step) - landed(idx)
                act.wait_ge(raw_full[s], at(16 * SLOT_LOADS[s], 16 * landed(idx)) + i * (16 * step))

            def split_hi(at, idx, i=0, per_step=0, main=BCOL, up=True, before=False, stack=False):
                s, w = idx % RAWS, wnum(idx)
                wait_raw(at, idx, i, per_step)
                act.wait_ge(slot_done[w % 2], at(PC_SPLIT, w // 2) + i * (per_step // 2))
                lo, hi = (0 if main else BCOL), (main or BCOL) + (P if up else 0)
                ins = rounded(whi[:, w % 2, lo:hi], raw[:, s, lo:hi])
                if before:
                    ins = factor_hi(whi[:, w % 2, DCOL:SPL].rearrange("p (b c) -> p b c", b=NB),
                                    raw[:, s, DCOL:RAW].rearrange("p (b r) -> p b r", b=NB), SCALE1)
                ins.then_inc(hi_done, 1)

            def rows_hi(at, n):
                act.wait_ge(t_full, at(N_T, n + 1))
                if n == TD:
                    act.wait_ge(prod_done, at(FT, FT))
                else:
                    act.wait_ge(r_done, at(N_T, n))
                for j in range(NB):
                    p, c = slice(GRP * j, GRP * (j + 1)), slice(BATCH * j, BATCH * (j + 1))
                    ins = rounded(scratch[p, c].bitcast(F32R), t_bank[n][p, c])
                ins.then_inc(h_ready, 1)

            def x_hi(par, m):
                rounded(xhi[:, m, :], res[:, par, m, :]).then_inc(a_hi, 1)

            def silu(at, f, i=0):
                w = wnum(I_GU + 2 * f)
                if isinstance(f, int) and f == FT - 1:
                    act.wait_ge(slot_done[1], at(PC_SPLIT, (w + 1) // 2 + 1))
                    p = slice(0, TAIL)
                else:
                    act.wait_ge(slot_done[0], at(PC_SPLIT, w // 2 + 1) + i * 2)
                    p = slice(0, P)
                if f == 0:
                    act.wait_ge(r_done, at(N_T, TU + 1))
                act.wait_ge(prod_done, at(FT, f) + i * 2)
                nc.scalar.activation(scratch[p, :], acc[2 * (f % 2)][p, :], ACT.Silu).then_inc(silu_done, 1)

            def hidden_hi(at, f, i=0):
                act.wait_ge(prod_done, at(FT, f + 1) + i * 2)
                if f < FULL:
                    dst = acthi[:, f, :] if isinstance(i, int) else acthi[:, bass.ds(i * 2 + f, 1), :].rearrange("p o n -> p (o n)")
                    rounded(dst, acc[2 * (f % 2) + 1][:]).then_inc(act_hi, 1)
                else:
                    rounded(tail[0:TAIL, :], acc[2][0:TAIL, :]).then_inc(act_hi, 1)

            with act.Fori(0, NTB // 2) as pair:
                for par in range(2):
                    at = At(pair, par)
                    wait_raw(at, I_AX)
                    act.wait_ge(t_full, at(N_T, 0))
                    for j in range(NB):
                        ins = factor_hi(ax0[:, :, GRP * j:GRP * (j + 1)],
                                        raw[:, 0, P * j:P * (j + 1)].rearrange("p (k r) -> p k r", r=RANK), SCALE0)
                    ins.then_inc(ax0_hi, 1)
                    act.wait_ge(x_full, at(16, 16))
                    for k in range(KH):
                        x_hi(par, k)
                    for j in range(NB):
                        ins = factor_hi(axp[:, :, :, GRP * j:GRP * (j + 1)].rearrange("p t k c -> p (t k) c"),
                                        raw[:, 0, 2 * P * (j + 1):2 * P * (j + 2)].rearrange("p (k r) -> p k r", r=RANK),
                                        SCALE1)
                    ins.then_inc(hi_done, 1)
                    split_hi(at, I_L0)
                    split_hi(at, I_L0 + 1)
                    rows_hi(at, T0)
                    for m in range(KH - 1):
                        split_hi(at, I_L0 + m + 2)
                    act.wait_ge(slot_done[1], at(PC_SPLIT, KH // 2))
                    for k in range(KH):
                        act.wait_ge(y_done, at(N_A, k + 1))
                        x_hi(par, k)
                    split_hi(at, I_GU + 1)
                    rows_hi(at, TG)
                    rows_hi(at, TU)
                    with act.Fori(0, (FT - 2) // 2) as i:
                        for f in range(2):
                            split_hi(at, I_GU + 2 * (f + 1), i, RAWS)
                            silu(at, f, i)
                            split_hi(at, I_GU + 2 * (f + 1) + 1, i, RAWS, before=True)
                            hidden_hi(at, f, i)
                    f = FT - 2
                    split_hi(at, I_GU + 2 * (f + 1))
                    silu(at, f)
                    split_hi(at, I_GU + 2 * (f + 1) + 1, main=0, before=True)
                    hidden_hi(at, f)
                    wait_raw(at, I_UV)
                    act.wait_ge(t_full, at(N_T, TU + 1))
                    for j in range(NB):
                        factor_hi(axp[:, :, :, GRP * j:GRP * (j + 1)].rearrange("p t k c -> p (t k) c"),
                                  raw[:, I_UV % RAWS, 2 * P * j:2 * P * (j + 1)].rearrange("p (k r) -> p k r", r=RANK),
                                  1.0)
                    factor_hi(ax0[:, 0, :].rearrange("p (b c) -> p b c", b=NB),
                              raw[:, I_UV % RAWS, DCOL:RAW].rearrange("p (b r) -> p b r", b=NB),
                              SCALE1).then_inc(hi_done, 1)
                    split_hi(at, I_DN, up=False)
                    silu(at, FT - 1)
                    split_hi(at, I_DN + 1, up=False)
                    hidden_hi(at, FT - 1)
                    for d in range(3 * KH):
                        m = d // 3
                        if d % 3 == 2:
                            act.wait_ge(y_done, at(N_A, KH + m + 1))
                            x_hi(par, m)
                        k = I_DN + d + 2
                        if k >= I_S2:
                            split_hi(at, k, up=False)
                        elif k % 3 == (I_DN + 2) % 3:
                            split_hi(at, k, main=DN_TILES[2] * P)
                        else:
                            split_hi(at, k, up=False)
                        if d == 0:
                            rows_hi(at, TD)
                    rows_hi(at, T2)
                    for m in range(KH):
                        act.wait_ge(y_done, at(N_A, 2 * KH + m + 1))
                        x_hi(par, m)
                    rows_hi(at, T3)

        @block.vector
        def _(dve):
            for n, r in enumerate((r0, r1, r2)):
                nc.vector.memset(r[:].bitcast(F32), 0.0).then_inc(zeroed, 1)
            dve.wait_ge(zeroed, 3)
            dve.wait_ge(const_in, 48)

            def factor_lo(dst, src, scale):
                return nc.vector.scalar_tensor_tensor(dst[:, :, 3 * RANK:GRP], src, scale,
                                                      dst[:, :, 0:RANK].bitcast(F32), ALU.mult, ALU.subtract)

            def split_lo(at, idx, i=0, per_step=0, main=BCOL, up=True, before=False, stack=False):
                s, b = idx % RAWS, wnum(idx) % 2
                dve.wait_ge(hi_done, at(NPIECE, idx + 1) + i * per_step)
                if main and not stack:
                    ins = nc.vector.tensor_tensor(wlo[:, b, 0:main], raw[:, s, 0:main],
                                                  whi[:, b, 0:main].bitcast(F32), ALU.subtract)
                if up or stack:
                    c = slice(0, BCOL) if stack else slice(main or BCOL, (main or BCOL) + P)
                    ins = nc.vector.scalar_tensor_tensor(whi[:, b, c], whi[:, b, c].bitcast(F32), mask_sb[:, 1:2],
                                                         raw[:, s, c], ALU.mult, ALU.add)
                if before:
                    ins = factor_lo(whi[:, b, DCOL:SPL].rearrange("p (b c) -> p b c", b=NB),
                                    raw[:, s, DCOL:RAW].rearrange("p (b r) -> p b r", b=NB), SCALE1)
                ins.then_inc(split_done[s], 1)

            def rows_lo(at, n):
                dve.wait_ge(h_ready, at(N_T, n + 1))
                for j in range(NB):
                    p, c = slice(GRP * j, GRP * (j + 1)), slice(BATCH * j, BATCH * (j + 1))
                    ins = nc.vector.scalar_tensor_tensor(t_rows[n][p, c], scratch[p, c], mask_sb[p, 0:1],
                                                         t_bank[n][p, c], ALU.mult, ALU.add)
                ins.then_inc(r_done, 1)

            def x_lo(at, par, layer, m):
                dve.wait_ge(a_hi, at(N_A, layer * KH + m + 1))
                nc.vector.tensor_tensor(xlo[:, m, :], res[:, par, m, :], xhi[:, m, :].bitcast(F32),
                                        ALU.subtract).then_inc(a_done, 1)

            def add_res(par, m):
                y = res[:, par, m, :]
                nc.vector.tensor_tensor(y, acc[m % 4][:], y, ALU.add).then_inc(y_done, 1)

            def product(at, f, i=0):
                if f == FT - 1:
                    dve.wait_ge(silu_done, at(FT, f + 1))
                    nc.vector.tensor_tensor(acc[2][0:TAIL, :], scratch[0:TAIL, :], acc[2][TAIL:P, :],
                                            ALU.mult).then_inc(prod_done, 1)
                else:
                    dve.wait_ge(silu_done, at(FT, f + 1) + i * 2)
                    w = wnum(I_GU + 2 * f + 1)
                    dve.wait_ge(slot_done[1], at(PC_SPLIT, w // 2 + 1) + i * 2)
                    up = acc[2 * (f % 2) + 1][:]
                    nc.vector.tensor_tensor(up, scratch[:], up, ALU.mult).then_inc(prod_done, 1)

            def hidden_lo(at, f, i=0):
                dve.wait_ge(act_hi, at(FT, f + 1) + i * 2)
                if f < FULL:
                    k = slice(f, f + 1) if isinstance(i, int) else bass.ds(i * 2 + f, 1)
                    lo = actlo[:, k, :].rearrange("p o n -> p (o n)")
                    hi = acthi[:, k, :].rearrange("p o n -> p (o n)")
                    nc.vector.tensor_tensor(lo, acc[2 * (f % 2) + 1][:], hi.bitcast(F32),
                                            ALU.subtract).then_inc(act_done, 1)
                else:
                    nc.vector.tensor_tensor(tail[TAIL:P, :], acc[2][0:TAIL, :], tail[0:TAIL, :].bitcast(F32),
                                            ALU.subtract).then_inc(act_done, 1)

            with dve.Fori(0, NTB // 2) as pair:
                for par in range(2):
                    at = At(pair, par)
                    dve.wait_ge(ax0_hi, at(1, 1))
                    for j in range(NB):
                        ins = factor_lo(ax0[:, :, GRP * j:GRP * (j + 1)],
                                        raw[:, 0, P * j:P * (j + 1)].rearrange("p (k r) -> p k r", r=RANK), SCALE0)
                    ins.then_inc(ax0_done, 1)
                    for k in range(KH):
                        x_lo(at, par, 0, k)
                    dve.wait_ge(hi_done, at(NPIECE, I_AX + 1))
                    for j in range(NB):
                        ins = factor_lo(axp[:, :, :, GRP * j:GRP * (j + 1)].rearrange("p t k c -> p (t k) c"),
                                        raw[:, 0, 2 * P * (j + 1):2 * P * (j + 2)].rearrange("p (k r) -> p k r", r=RANK),
                                        SCALE1)
                    ins.then_inc(split_done[0], 1)
                    split_lo(at, I_L0)
                    split_lo(at, I_L0 + 1)
                    rows_lo(at, T0)
                    for m in range(KH):
                        dve.wait_ge(slot_done[m % 2], at(PC_SPLIT, m // 2 + 1))
                        y = res[:, par, m, :]
                        nc.vector.scalar_tensor_tensor(y, acc[m % 4][:], bias_sb[:, m:m + 1], y,
                                                       ALU.add, ALU.add).then_inc(y_done, 1)
                        if m < KH - 1:
                            split_lo(at, I_L0 + m + 2)
                    for k in range(KH):
                        x_lo(at, par, 1, k)
                    split_lo(at, I_GU + 1)
                    rows_lo(at, TG)
                    rows_lo(at, TU)
                    with dve.Fori(0, (FT - 2) // 2) as i:
                        for f in range(2):
                            split_lo(at, I_GU + 2 * (f + 1), i, RAWS)
                            product(at, f, i)
                            split_lo(at, I_GU + 2 * (f + 1) + 1, i, RAWS, before=True)
                            hidden_lo(at, f, i)
                    f = FT - 2
                    split_lo(at, I_GU + 2 * (f + 1))
                    product(at, f)
                    split_lo(at, I_GU + 2 * (f + 1) + 1, main=0, before=True)
                    hidden_lo(at, f)
                    dve.wait_ge(hi_done, at(NPIECE, I_UV + 1))
                    for j in range(NB):
                        factor_lo(axp[:, :, :, GRP * j:GRP * (j + 1)].rearrange("p t k c -> p (t k) c"),
                                  raw[:, I_UV % RAWS, 2 * P * j:2 * P * (j + 1)].rearrange("p (k r) -> p k r", r=RANK),
                                  1.0)
                    factor_lo(ax0[:, 0, :].rearrange("p (b c) -> p b c", b=NB),
                              raw[:, I_UV % RAWS, DCOL:RAW].rearrange("p (b r) -> p b r", b=NB),
                              SCALE1).then_inc(split_done[I_UV % RAWS], 1)
                    split_lo(at, I_DN, up=False)
                    product(at, FT - 1)
                    split_lo(at, I_DN + 1, up=False)
                    hidden_lo(at, FT - 1)
                    for d in range(3 * KH):
                        m = d // 3
                        if d % 3 == 2:
                            w = wnum(I_DN + d)
                            dve.wait_ge(slot_done[w % 2], at(PC_SPLIT, w // 2 + 1))
                            add_res(par, m)
                            x_lo(at, par, 2, m)
                        k = I_DN + d + 2
                        if k >= I_S2:
                            split_lo(at, k, up=False, stack=True)
                        elif k % 3 == (I_DN + 2) % 3:
                            split_lo(at, k, main=DN_TILES[2] * P)
                        else:
                            split_lo(at, k, up=False)
                        if d == 0:
                            rows_lo(at, TD)
                    for layer in range(2):
                        rows_lo(at, T2 + layer)
                        for m in range(KH):
                            if m < KH - 1:
                                dve.wait_ge(s_acc, at(2 * (KH - 1), layer * (KH - 1) + m + 1))
                            else:
                                dve.wait_ge(slot_done[layer], at(PC_SPLIT, PC_SPLIT))
                            add_res(par, m)
                            if layer == 0 and m:
                                x_lo(at, par, 3, m - 1)
                        if layer == 0:
                            x_lo(at, par, 3, KH - 1)

        @block.tensor
        def _(pe):
            def mm(dst, stationary, moving, start, stop):
                return pe.matmul(dst, stationary, moving, start=start, stop=stop)

            def wait_piece(at, idx, i=0, per_step=0):
                s = idx % RAWS
                pe.wait_ge(split_done[s], at(PC_RAW, idx // RAWS + 1) + i * (per_step // RAWS))

            def thrice(dst, b, j, hi, lo, start):
                c = slice(j * P, (j + 1) * P)
                mm(dst, whi[:, b, c], hi, start, False)
                mm(dst, whi[:, b, c], lo, False, False)
                return mm(dst, wlo[:, b, c], hi, False, False)

            def width(dst, b):
                for k in range(KH):
                    ins = thrice(dst, b, k, xhi[:, k, :], xlo[:, k, :], k == 0)
                return ins

            def down_factor(at, layer, n, factor):
                for k in range(KH):
                    pe.wait_ge(a_done, at(N_A, layer * KH + k + 1))
                    mm(t_bank[n][:], factor[:, k, :], xhi[:, k, :], k == 0, False)
                    ins = mm(t_bank[n][:], factor[:, k, :], xlo[:, k, :], False, k == KH - 1)
                ins.then_inc(t_full, 1)

            def hidden_down(at, f, stationary, i=0):
                pe.wait_ge(act_done, at(FT, f + 1) + i * 2)
                if f < FULL:
                    k = slice(f, f + 1) if isinstance(i, int) else bass.ds(i * 2 + f, 1)
                    mm(t_bank[TD][:], stationary, acthi[:, k, :].rearrange("p o n -> p (o n)"), f == 0, False)
                    return mm(t_bank[TD][:], stationary, actlo[:, k, :].rearrange("p o n -> p (o n)"), False, False)
                return mm(t_bank[TD][:], stationary, tail[:], False, True)

            def gate_up(at, h, i, f0, first=False, before=True):
                f = f0 + h
                g = I_GU + 2 * f
                gate, up = acc[2 * (f % 2)][:], acc[2 * (f % 2) + 1][:]
                if not first:
                    pe.wait_ge(act_done, at(FT, f - 1) + i * 2)
                wait_piece(at, g, i, RAWS)
                width(gate, 0)
                mm(gate, whi[:, 0, BCOL:DCOL], r1[:], False, f < FT - 1).then_inc(slot_done[0], 1)
                wait_piece(at, g + 1, i, RAWS)
                if f < FT - 1:
                    width(up, 1)
                    ins = mm(up, whi[:, 1, BCOL:DCOL], r2[:], False, True)
                else:
                    ins = mm(gate, whi[:, 1, BCOL:DCOL], r2[:], False, True)
                if before:
                    ins = hidden_down(at, f - 1, whi[:, 1, DCOL:SPL], i)
                ins.then_inc(slot_done[1], 1)

            with pe.Fori(0, NTB // 2) as pair:
                for par in range(2):
                    at = At(pair, par)
                    pe.wait_ge(ax0_done, at(1, 1))
                    down_factor(at, 0, T0, ax0)
                    with pe.Fori(0, KH // RAWS) as i:
                        for m in range(RAWS):
                            pe.wait_ge(y_done, at(N_A, 0) + i * (m + 1))
                            wait_piece(at, I_L0 + m, i, RAWS)
                            width(acc[m][:], m % 2)
                            if m == 0:
                                pe.wait_ge(r_done, at(N_T, T0 + 1))
                            mm(acc[m][:], whi[:, m % 2, BCOL:DCOL], r0[:], False, True).then_inc(slot_done[m % 2], 1)
                    wait_piece(at, I_AX)
                    down_factor(at, 1, TG, axp[:, 0])
                    down_factor(at, 1, TU, axp[:, 1])
                    pe.wait_ge(y_done, at(N_A, KH))
                    pe.wait_ge(r_done, at(N_T, TU + 1))
                    gate_up(at, 0, 0, 0, first=True, before=False)
                    gate_up(at, 1, 0, 0, first=True)
                    with pe.Fori(0, (FT - 4) // 2) as i:
                        for h in range(2):
                            gate_up(at, h, i, 2)
                    gate_up(at, 0, 0, FT - 2)
                    gate_up(at, 1, 0, FT - 2)
                    for m in range(KH):
                        dst = acc[m % 4][:]
                        if m >= 4:
                            pe.wait_ge(y_done, at(N_A, KH + m - 3))
                        else:
                            pe.wait_ge(act_done, at(FT, FT - 1 + m // 2))
                        for q, tiles in enumerate(DN_TILES):
                            k = I_DN + 3 * m + q
                            b = wnum(k) % 2
                            wait_piece(at, k)
                            for j in range(tiles):
                                f = sum(DN_TILES[:q]) + j
                                if f < FULL:
                                    ins = thrice(dst, b, j, acthi[:, f, :], actlo[:, f, :], f == 0)
                                else:
                                    pe.wait_ge(act_done, at(FT, FT))
                                    mm(dst, whi[:, b, j * P:(j + 1) * P], tail[:], False, False)
                                    mm(dst, wlo[:, b, j * P:(j + 1) * P], tail[:], False, False)
                            if q == 2:
                                pe.wait_ge(r_done, at(N_T, TD + 1))
                                ins = mm(dst, whi[:, b, tiles * P:(tiles + 1) * P], r0[:], False, True)
                            ins.then_inc(slot_done[b], 1)
                            if m == 0 and q == 0:
                                wait_piece(at, I_UV)
                                hidden_down(at, FT - 1, ax0[:, 0, :]).then_inc(t_full, 1)
                    for layer in range(2):
                        down_factor(at, 2 + layer, T2 + layer, axp[:, layer])
                        wait_piece(at, I_S2 + layer)
                        pe.wait_ge(r_done, at(N_T, T2 + layer + 1))
                        for m in range(KH):
                            pe.wait_ge(y_done, at(N_A, (2 + layer) * KH + m - 3))
                            ins = mm(acc[m % 4][:], whi[:, layer, m * P:(m + 1) * P], t_rows[T2 + layer][:], True, True)
                            ins.then_inc(s_acc if m < KH - 1 else slot_done[layer], 1)


def kernel(**inputs):
    import concourse.bacc as bacc
    from concourse.bass_utils import run_bass_kernel_spmd

    a = {k: np.ascontiguousarray(v) for k, v in inputs.items()}

    def chunks(w):
        n, k, m = w.shape
        return w.reshape(n, k // P, P, m).transpose(0, 2, 1, 3).reshape(n, P, k // P * m)

    def four(w):
        return np.concatenate([w] * 4, axis=1)

    def tiles(w):
        n, r, c = w.shape
        return w.reshape(n, r, c // P, P).transpose(0, 2, 1, 3)

    x = a["x"].reshape(NTB, TB, KH, P).transpose(0, 3, 2, 1).reshape(NTB, P, KH * TB)
    w0 = chunks(a["L0_cond_W"].reshape(KH, P, H).transpose(0, 2, 1))
    gate, up = a["L1_cond_W_gate"], a["L1_cond_W_up"]
    gu = np.stack([gate[:FULL * P].reshape(FULL, P, H), up[:FULL * P].reshape(FULL, P, H)], axis=1)
    gu = gu.reshape(2 * FULL, P, H)
    gu = np.concatenate([gu, np.concatenate([gate[FULL * P:], up[FULL * P:]])[None]])
    wgu = chunks(gu.transpose(0, 2, 1))
    dt = a["L1_cond_W_down"].T
    dt = np.concatenate([dt, dt[FULL * P:]])
    wdn = chunks(dt.reshape(FT * P, KH, P).transpose(1, 0, 2))
    a0 = chunks(a["L0_cond_lora_As"])
    agu = np.concatenate([chunks(a["L1_cond_A_gate"][0].transpose(0, 2, 1)),
                          chunks(a["L1_cond_A_up"][0].transpose(0, 2, 1))], axis=2)
    b0 = tiles(four(a["L0_cond_lora_Bs"]))
    bgt = a["L1_cond_B_gate"][0].transpose(0, 2, 1)
    but = a["L1_cond_B_up"][0].transpose(0, 2, 1)
    zero = np.zeros_like(bgt[:, :, :TAIL])
    bg = tiles(four(np.concatenate([bgt, zero], axis=2)))
    bu = tiles(four(np.concatenate([but[:, :, :FULL * P], zero, but[:, :, FULL * P:]], axis=2)))
    adt = a["L1_cond_A_down"][0].transpose(0, 2, 1)
    adt = np.concatenate([adt, adt[:, FULL * P:]], axis=1)
    ad = adt.reshape(adt.shape[0], FT, P, RANK)
    bd = tiles(four(a["L1_cond_B_down"][0].transpose(0, 2, 1)))
    uf = chunks(a["L2_cond_B"].transpose(0, 2, 1))
    vf = chunks(a["L3_cond_B"].transpose(0, 2, 1))
    s2 = four(a["L2_cond_A"].transpose(0, 2, 1))
    s3 = four(a["L3_cond_A"].transpose(0, 2, 1))
    bias = a["L0_cond_b"].reshape(KH, P).T
    ids = np.stack([a[n].reshape(NTB, NB) for n in ("itok_B_0_23", "itok_B_2_6", "itok_B_4_50", "itok_B_3_7")], axis=1)
    ids = ids.reshape(1, NTB * 4 * NB)
    masks = np.zeros((P, 2), np.float32)
    masks[np.arange(P) // RANK % 4 == 1, 0] = -1.0
    masks[np.arange(P) // RANK % 4 == 2, 1] = -1.0

    names = ("x", "bias", "idx", "w0", "wgu", "wdn", "a0", "agu", "b0", "bg", "bu", "ad", "bd", "uf", "vf", "s2", "s3",
             "masks")
    given = (x, bias, ids, w0, wgu, wdn, a0, agu, b0, bg, bu, ad, bd, uf, vf, s2, s3, masks)
    nc = bacc.Bacc("TRN2", target_bir_lowering=False, num_devices=1)
    arrays, args = {}, []
    for name, v in zip(names, given):
        v = np.ascontiguousarray(v)
        arrays[f"in_{name}"] = v
        args.append(nc.dram_tensor(f"in_{name}", v.shape, mybir.dt.from_np(v.dtype), kind="ExternalInput").ap())
    out = nc.dram_tensor("out_y", (NTB, KH, P, TB), F32, kind="ExternalOutput").ap()
    adapted_layers(nc, *args, out)
    got = run_bass_kernel_spmd(nc, [arrays], core_ids=[0]).results[0]["out_y"]
    return got.transpose(0, 3, 1, 2).reshape(TOKENS // BATCH, BATCH, H)
```

```python
from contextlib import ExitStack

import numpy as np

import concourse.bass as bass
from concourse import mybir

ALU = mybir.AluOpType
ACT = mybir.ActivationFunctionType
F32 = mybir.dt.float32
F32R = mybir.dt.float32r
I32 = mybir.dt.int32

P = 128
TOKENS, H, F, RANK = 2048, 1024, 2752, 16
BATCH = 256
TB = 512
NTB = TOKENS // TB
NB = TB // BATCH
KH = H // P
FULL = F // P
FT = FULL + 1
TAIL = F - FULL * P
GRP = 4 * RANK
SCALE0, SCALE1 = 2.0, 0.5

I_A0 = 0
I_L0 = 1
I_AG = I_L0 + KH
I_GU = I_AG + 1
I_LAST_UP = I_GU + 2 * FT - 1
I_DN = I_GU + 2 * FT
I_S2 = I_DN + 3 * KH
I_S3 = I_S2 + 1
NPIECE = I_S3 + 1
RAWS = 4
assert NPIECE % RAWS == 0 and TAIL * 2 == P

BCOL = KH * P
DCOL = BCOL + P
RAW = DCOL + NB * RANK
SPL = DCOL + P
UVCOL = 2 * P * NB
DN_TILES = (8, 8, 6)

LOADS = [0] * NPIECE
LOADS[I_A0] = LOADS[I_AG] = NB
for _m in range(KH):
    LOADS[I_L0 + _m] = 1 + NB
for _f in range(FT):
    LOADS[I_GU + 2 * _f] = 1 + NB
    LOADS[I_GU + 2 * _f + 1] = 1 + NB + (NB if _f else 0)
LOADS[I_LAST_UP] = 5 * NB
for _m in range(KH):
    LOADS[I_DN + 3 * _m] = LOADS[I_DN + 3 * _m + 1] = 1
    LOADS[I_DN + 3 * _m + 2] = 1 + NB
LOADS[I_S2] = LOADS[I_S3] = NB
SLOT_LOADS = [sum(LOADS[s::RAWS]) for s in range(RAWS)]


def landed(idx):
    return sum(LOADS[idx % RAWS:idx + 1:RAWS])


def wnum(idx):
    return idx - 1 if idx < I_AG else idx - 2 if idx <= I_LAST_UP else idx - 3


NW = wnum(I_S2)

PC_RAW = NPIECE // RAWS
PC_SPLIT = ((NW + 1) // 2, NW // 2)
N_A = 3 * KH


class At:
    def __init__(self, t, off=0):
        self.t, self.off = t, off

    def __call__(self, per_block, n):
        return self.t * per_block + (self.off * per_block + n)


FIRST_X4 = 10
V_ROWS = 9
FIRST_K = 2


def adapted_layers(nc, x, bias, idx, w0, wgu, wdn, a0, agu, b0, bg, bu, ad, bd, uf, vf, s2, s3, masks, out):
    with ExitStack() as ctx:
        def sb(name, shape, dt):
            return ctx.enter_context(nc.sbuf_tensor(name, shape, dt))

        def sem(name):
            return ctx.enter_context(nc.semaphore(name))

        xhi = sb("xhi", [P, KH, TB], F32R)
        xlo = sb("xlo", [P, KH, TB], F32R)
        acthi = sb("acthi", [P, FULL, TB], F32R)
        actlo = sb("actlo", [P, FULL, TB], F32R)
        tail = sb("tail", [P, TB], F32R)
        res = sb("res", [P, KH, TB], F32)
        res2 = sb("res2", [P, KH, TB], F32)
        x3hi = sb("x3hi", [P, 2, TB], F32R)
        x3lo = sb("x3lo", [P, 2, TB], F32R)
        ax0 = sb("ax0", [P, KH, P], F32R)
        axp = sb("axp", [P, 2, KH, P], F32R)
        bx = sb("bx", [P, 2, BCOL], F32R)
        r0 = sb("r0", [P, TB], F32R)
        r1 = sb("r1", [P, TB], F32R)
        r2 = sb("r2", [P, TB], F32R)
        scratch = sb("scratch", [P, TB], F32)
        whi = sb("whi", [P, 2, SPL], F32R)
        wlo = sb("wlo", [P, 2, BCOL], F32R)
        raw = sb("raw", [P, RAWS, RAW], F32)
        bias_sb = sb("bias_sb", [P, KH], F32)
        mask_sb = sb("mask_sb", [P, 2], F32)
        idx_sb = sb("idx_sb", [1, NTB * 4 * NB], I32)
        acc = [ctx.enter_context(nc.psum_tensor(f"acc{i}", [P, TB], F32)) for i in range(4)]
        tps = [ctx.enter_context(nc.psum_tensor(f"tps{i}", [P, TB], F32)) for i in range(4)]
        T0, TG, TU, TD, T2, T3 = range(6)
        t_bank = [tps[0], tps[1], tps[2], tps[3], tps[1], tps[2]]
        t_rows = [r0, r1, r2, r0, r1, r2]
        t_copy = [scratch[:]] * 5 + [x3hi[:, 0, :].bitcast(F32)]
        x3_bank = [tps[3], tps[1]]
        x4_bank = [tps[3], tps[1], tps[0]]

        idx_in = sem("idx_in")
        const_in = sem("const_in")
        zeroed = sem("zeroed")
        x_full = [sem(f"x_full{k}") for k in range(KH)]
        raw_full = [sem(f"raw_full{s}") for s in range(RAWS)]
        hi_done = sem("hi_done")
        split_done = [sem(f"split_done{s}") for s in range(RAWS)]
        slot_done = [sem(f"slot_done{s}") for s in range(2)]
        last_up_done = sem("last_up_done")
        t_full = [sem(f"t_full{n}") for n in range(6)]
        h_ready = [sem(f"h_ready{n}") for n in range(6)]
        r_done = [sem(f"r_done{n}") for n in range(6)]
        x_used = sem("x_used")
        a_hi = sem("a_hi")
        a_done = sem("a_done")
        x1_done = sem("x1_done")
        x2_done = sem("x2_done")
        x3_done = sem("x3_done")
        x4_done = sem("x4_done")
        x3_sum = sem("x3_sum")
        x4_sum = sem("x4_sum")
        x3_hi = sem("x3_hi")
        x3_split = sem("x3_split")
        x3_used = sem("x3_used")
        silu_done = sem("silu_done")
        prod_done = sem("prod_done")
        act_hi = sem("act_hi")
        act_done = sem("act_done")
        out_done = sem("out_done")

        block = ctx.enter_context(nc.Block())

        @block.sync
        def _(sp):
            def load_piece(at, idx0, step, per_step, parts):
                s = idx0 % RAWS
                n = at(PC_RAW, idx0 // RAWS)
                if not (isinstance(n, int) and n == 0):
                    sp.wait_ge(split_done[s], n + step * (per_step // RAWS))
                for dst, src in parts:
                    sp.dma_start(dst(s), src).then_inc(raw_full[s], 16)

            def cols(a, b):
                return lambda s: raw[:, s, a:b]

            def rows(j, a, b):
                return lambda s: raw[GRP * j:GRP * (j + 1), s, a:b]

            def of(array, i):
                return array[bass.ds(i, 1)].rearrange("o p c -> (o p) c")

            def of2(array, i, k):
                return array[bass.ds(i, 1), bass.ds(k, 1)].rearrange("o q p c -> (o q p) c")

            def adapter(t, kind, top):
                return [sp.value_load(idx_sb[0:1, bass.ds(t * (4 * NB) + (NB * kind + j), 1)],
                                      min_val=0, max_val=top.shape[0] - 1) for j in range(NB)]

            def a0_piece(at, e0):
                load_piece(at, I_A0, 0, 0, [(cols(P * j, P * (j + 1)), of(a0, e0[j])) for j in range(NB)])

            def l0_piece(at, i, m, e0):
                load_piece(at, I_L0 + m, i, RAWS,
                           [(cols(0, BCOL), of(w0, i * RAWS + m))]
                           + [(rows(j, BCOL, DCOL), of2(b0, e0[j], i * RAWS + m)) for j in range(NB)])

            def gate_up(at, i, f0, e1, before=(True, True)):
                for h in range(2):
                    f = i * 2 + (f0 + h)
                    g = i * 4 + 2 * (f0 + h)
                    k = I_GU + 2 * (f0 + h)
                    load_piece(at, k, i, RAWS,
                               [(cols(0, BCOL), of(wgu, g))]
                               + [(rows(j, BCOL, DCOL), of2(bg, e1[j], f)) for j in range(NB)])
                    if k + 1 < I_LAST_UP:
                        load_piece(at, k + 1, i, RAWS,
                                   [(cols(0, BCOL), of(wgu, g + 1))]
                                   + [(rows(j, BCOL, DCOL), of2(bu, e1[j], f)) for j in range(NB)]
                                   + ([(cols(DCOL + RANK * j, DCOL + RANK * (j + 1)), of2(ad, e1[j], f - 1))
                                       for j in range(NB)] if before[h] else []))

            def mid(t, at):
                e1, e2, e3 = adapter(t, 1, agu), adapter(t, 2, uf), adapter(t, 3, vf)
                load_piece(at, I_AG, 0, 0, [(cols(2 * P * j, 2 * P * (j + 1)), of(agu, e1[j])) for j in range(NB)])
                gate_up(at, 0, 0, e1, (False, True))
                with sp.Fori(0, (FT - 4) // 2) as i:
                    gate_up(at, i, 2, e1)
                gate_up(at, 0, FT - 2, e1)
                load_piece(at, I_LAST_UP, 0, 0,
                           [(rows(j, BCOL, DCOL), of2(bu, e1[j], FT - 1)) for j in range(NB)]
                           + [(cols(DCOL + RANK * j, DCOL + RANK * (j + 1)), of2(ad, e1[j], FT - 2)) for j in range(NB)]
                           + [(cols(2 * P * j, 2 * P * j + P), of(uf, e2[j])) for j in range(NB)]
                           + [(cols(2 * P * j + P, 2 * P * j + 2 * P), of(vf, e3[j])) for j in range(NB)]
                           + [(cols(UVCOL + RANK * j, UVCOL + RANK * (j + 1)), of2(ad, e1[j], FT - 1))
                              for j in range(NB)])
                with sp.Fori(0, 2) as i:
                    for m in range(4):
                        for q in range(3):
                            w = DN_TILES[q] * P
                            c = sum(DN_TILES[:q]) * P
                            load_piece(at, I_DN + 3 * m + q, i, 3 * 4,
                                       [(cols(0, w), of(wdn, i * 4 + m)[:, c:c + w])]
                                       + ([(rows(j, w, w + P), of2(bd, e1[j], i * 4 + m)) for j in range(NB)]
                                          if q == 2 else []))
                load_piece(at, I_S2, 0, 0, [(rows(j, 0, BCOL), of(s2, e2[j])) for j in range(NB)])
                load_piece(at, I_S3, 0, 0, [(rows(j, 0, BCOL), of(s3, e3[j])) for j in range(NB)])

            sp.dma_start(idx_sb[:], idx).then_inc(idx_in, 16)
            sp.dma_start(bias_sb[:], bias).then_inc(const_in, 16)
            sp.dma_start(mask_sb[:], masks).then_inc(const_in, 16)
            sp.dma_start(res[:, 0, :], x[0, 0]).then_inc(x_full[0], 16)
            sp.wait_ge(idx_in, 16)
            at = At(0)
            e0 = adapter(0, 0, a0)
            a0_piece(at, e0)
            for m in range(KH):
                l0_piece(at, 0, m, e0)
                if m == 0:
                    for k in range(1, KH):
                        sp.dma_start(res[:, k, :], x[0, k]).then_inc(x_full[k], 16)
            with sp.Fori(0, NTB - 1) as t:
                mid(t, At(t))
                e0 = adapter(t + 1, 0, a0)
                a0_piece(At(t, 1), e0)
                with sp.Fori(0, KH // RAWS) as i:
                    for m in range(RAWS):
                        l0_piece(At(t, 1), i, m, e0)
            mid(NTB - 1, At(NTB - 1))

        @block.gpsimd
        def _(pool):
            with pool.Fori(0, NTB) as t:
                at = At(t)
                for s in range(KH):
                    pool.wait_ge(x3_hi, at(KH, s + 1))
                    nc.gpsimd.tensor_tensor(x3lo[:, s % 2, :], res2[:, s, :], x3hi[:, s % 2, :].bitcast(F32),
                                            ALU.subtract).then_inc(x3_split, 1)

        @block.scalar
        def _(act):
            def rounded(dst, src, scale=1.0):
                return nc.scalar.activation(dst, src, ACT.Copy, scale=scale)

            def factor_hi(dst, src, scale):
                n = src.shape[1]
                return rounded(dst[:, :, 0:3 * RANK].rearrange("p n (g r) -> p n g r", g=3),
                               src.unsqueeze(2).to_broadcast([P, n, 3, RANK]), scale)

            def pair_hi(s, scale):
                for j in range(NB):
                    ins = factor_hi(axp[:, :, :, GRP * j:GRP * (j + 1)].rearrange("p t k c -> p (t k) c"),
                                    raw[:, s, 2 * P * j:2 * P * (j + 1)].rearrange("p (k r) -> p k r", r=RANK), scale)
                return ins

            def wait_raw(at, idx, i=0, per_step=0):
                s = idx % RAWS
                step = landed(idx + per_step) - landed(idx)
                act.wait_ge(raw_full[s], at(16 * SLOT_LOADS[s], 16 * landed(idx)) + i * (16 * step))

            def split_hi(at, idx, i=0, per_step=0, main=BCOL, up=True, before=False, last=True):
                s, w = idx % RAWS, wnum(idx)
                wait_raw(at, idx, i, per_step)
                n = at(PC_SPLIT[w % 2], w // 2)
                if not (isinstance(n, int) and n == 0):
                    act.wait_ge(slot_done[w % 2], n + i * (per_step // 2))
                lo, hi = (0 if main else BCOL), (main or BCOL) + (P if up else 0)
                ins = rounded(whi[:, w % 2, lo:hi], raw[:, s, lo:hi])
                if before:
                    ins = factor_hi(whi[:, w % 2, DCOL:SPL].rearrange("p (b c) -> p b c", b=NB),
                                    raw[:, s, DCOL:RAW].rearrange("p (b r) -> p b r", b=NB), SCALE1)
                if last:
                    ins.then_inc(hi_done, 1)

            def rows_hi(at, n, sem_before, value):
                if n == T2:
                    act.wait_ge(x_used, at(2 * KH, 2 * KH))
                else:
                    act.wait_ge(t_full[n], at(1, 1))
                if sem_before is not None:
                    act.wait_ge(sem_before, value)
                for j in range(NB):
                    p, c = slice(GRP * j, GRP * (j + 1)), slice(BATCH * j, BATCH * (j + 1))
                    ins = rounded(t_copy[n][p, c].bitcast(F32R), t_bank[n][p, c])
                ins.then_inc(h_ready[n], 1)

            def x_hi(src, k):
                rounded(xhi[:, k, :], src[:, k, :]).then_inc(a_hi, 1)

            def silu(at, f, i=0):
                w = wnum(I_GU + 2 * f)
                if f == FT - 1:
                    act.wait_ge(last_up_done, at(1, 1))
                    p = slice(0, TAIL)
                else:
                    act.wait_ge(slot_done[0], at(PC_SPLIT[0], w // 2 + 1) + i * 2)
                    p = slice(0, P)
                if f == 0:
                    act.wait_ge(r_done[TU], at(1, 1))
                act.wait_ge(prod_done, at(FT, f + 1) + i * 2)
                nc.scalar.activation(scratch[p, :], acc[2 * (f % 2)][p, :], ACT.Silu).then_inc(silu_done, 1)

            def hidden_hi(at, f, i=0):
                act.wait_ge(prod_done, at(FT, f + 2) + i * 2)
                if f < FULL:
                    k = slice(f, f + 1) if isinstance(i, int) else bass.ds(i * 2 + f, 1)
                    rounded(acthi[:, k, :].rearrange("p o n -> p (o n)"), acc[2 * (f % 2) + 1][:]).then_inc(act_hi, 1)
                else:
                    rounded(tail[0:TAIL, :], acc[2][0:TAIL, :]).then_inc(act_hi, 1)

            def a0_hi(at):
                wait_raw(at, I_A0)
                for j in range(NB):
                    ins = factor_hi(ax0[:, :, GRP * j:GRP * (j + 1)],
                                    raw[:, I_A0, P * j:P * (j + 1)].rearrange("p (k r) -> p k r", r=RANK), SCALE0)
                ins.then_inc(hi_done, 1)

            def x3_chunk(at, s):
                act.wait_ge(x3_done, at(KH, s + 1))
                if s >= 2:
                    act.wait_ge(x3_used, at(KH - 1, s - 1))
                rounded(x3hi[:, s % 2, :], res2[:, s, :]).then_inc(x3_hi, 1)

            def store_pair(t, at, j):
                for m in (2 * j, 2 * j + 1):
                    act.wait_ge(x4_done, at(KH, m + 1))
                    act.dma_start(out[bass.ds(t, 1), m].rearrange("o p c -> (o p) c"), res2[:, m, :]).then_inc(out_done, 16)

            def last_layers(t, at, h):
                if 0 <= h + 1 < KH:
                    x3_chunk(at, h + 1)
                if h == V_ROWS:
                    rows_hi(at, T3, None, 0)
                if 0 <= h - FIRST_X4 - 1 < KH // 2:
                    store_pair(t, at, h - FIRST_X4 - 1)

            def head(at, prev=None):
                for k in range(KH):
                    act.wait_ge(x_full[k], at(16, 16))
                    if prev:
                        act.wait_ge(x_used, prev[1](2 * KH, KH + k + 1))
                    x_hi(res, k)
                    if k == FIRST_K - 1:
                        split_hi(at, I_L0)
                    if prev and k == 5:
                        rows_hi(prev[1], T2, r_done[TD], prev[1](1, 1))
                split_hi(at, I_L0 + 1)
                if prev:
                    rows_hi(at, T0, r_done[T2], prev[1](1, 1))
                    last_layers(*prev, -1)
                else:
                    rows_hi(at, T0, None, 0)
                for m in range(KH):
                    if m and prev:
                        last_layers(*prev, 2 * m - 2)
                        last_layers(*prev, 2 * m - 1)
                    if m == KH - 2:
                        wait_raw(at, I_AG)
                        act.wait_ge(slot_done[1], at(PC_SPLIT[1], 3))
                        pair_hi(I_AG % RAWS, SCALE1).then_inc(hi_done, 1)
                        split_hi(at, I_GU)
                    elif m < KH - 2:
                        split_hi(at, I_L0 + m + 2)
                if prev:
                    last_layers(*prev, 2 * KH - 2)

            def mid(t, at, more):
                for k in range(KH):
                    act.wait_ge(x1_done, at(KH, k + 1))
                    act.wait_ge(x_used, at(2 * KH, k + 1))
                    x_hi(res, k)
                split_hi(at, I_GU + 1)
                rows_hi(at, TG, r_done[T0], at(1, 1))
                rows_hi(at, TU, r_done[TG], at(1, 1))
                with act.Fori(0, (FT - 2) // 2) as i:
                    for f in range(2):
                        split_hi(at, I_GU + 2 * (f + 1), i, RAWS)
                        silu(at, f, i)
                        split_hi(at, I_GU + 2 * (f + 1) + 1, i, RAWS, before=True)
                        hidden_hi(at, f, i)
                f = FT - 2
                split_hi(at, I_GU + 2 * (f + 1))
                silu(at, f)
                split_hi(at, I_LAST_UP, main=0, before=True, last=False)
                act.wait_ge(t_full[TU], at(1, 1))
                s = I_LAST_UP % RAWS
                pair_hi(s, 1.0)
                factor_hi(ax0[:, 0, :].rearrange("p (b c) -> p b c", b=NB),
                          raw[:, s, UVCOL:UVCOL + NB * RANK].rearrange("p (b r) -> p b r", b=NB),
                          SCALE1).then_inc(hi_done, 1)
                split_hi(at, I_DN, up=False)
                hidden_hi(at, f)
                split_hi(at, I_DN + 1, up=False)
                silu(at, FT - 1)
                hidden_hi(at, FT - 1)
                for d in range(3 * KH):
                    m = d // 3
                    if d % 3 == 2:
                        act.wait_ge(x2_done, at(KH, m + 1))
                        x_hi(res2, m)
                        if more:
                            act.dma_start(res[:, m, :], x[bass.ds(t + 1, 1), m].rearrange("o p c -> (o p) c")
                                          ).then_inc(x_full[m], 16)
                    if d + 2 < 3 * KH:
                        q = (d + 2) % 3
                        split_hi(at, I_DN + d + 2, main=DN_TILES[q] * P, up=q == 2)
                    if d == 0:
                        rows_hi(at, TD, prod_done, at(FT, FT + 1))
                    if d == 3 * KH - 3:
                        for k in (I_S2, I_S3):
                            wait_raw(at, k)
                            rounded(bx[:, k - I_S2, :], raw[:, k % RAWS, 0:BCOL]).then_inc(hi_done, 1)
                    if more and d == 3 * KH - 3:
                        a0_hi(At(at.t, at.off + 1))

            act.sem_inc(out_done, 16)
            act.wait_ge(zeroed, 1)
            nc.scalar.activation(scratch[:, 0:1], r0[:, 0:1].bitcast(F32), ACT.Silu)
            a0_hi(At(0))
            head(At(0))
            with act.Fori(0, NTB - 1) as t:
                mid(t, At(t), True)
                head(At(t, 1), (t, At(t)))
            t, at = NTB - 1, At(NTB - 1)
            mid(t, at, False)
            rows_hi(at, T2, r_done[TD], at(1, 1))
            for h in range(-1, FIRST_X4 + KH // 2 + 1):
                last_layers(t, at, h)
            act.wait_ge(out_done, 16 + 16 * KH * NTB)

        @block.vector
        def _(dve):
            def factor_lo(dst, src, scale):
                return nc.vector.scalar_tensor_tensor(dst[:, :, 3 * RANK:GRP], src, scale,
                                                      dst[:, :, 0:RANK].bitcast(F32), ALU.mult, ALU.subtract)

            def pair_lo(s, scale):
                for j in range(NB):
                    ins = factor_lo(axp[:, :, :, GRP * j:GRP * (j + 1)].rearrange("p t k c -> p (t k) c"),
                                    raw[:, s, 2 * P * j:2 * P * (j + 1)].rearrange("p (k r) -> p k r", r=RANK), scale)
                return ins

            def up_rows(dst, src):
                return nc.vector.scalar_tensor_tensor(dst, dst.bitcast(F32), mask_sb[:, 1:2], src, ALU.mult, ALU.add)

            def split_lo(at, idx, i=0, per_step=0, main=BCOL, up=True, before=False, last=True):
                s, b = idx % RAWS, wnum(idx) % 2
                dve.wait_ge(hi_done, at(NPIECE, idx + 1) + i * per_step)
                if main:
                    ins = nc.vector.tensor_tensor(wlo[:, b, 0:main], raw[:, s, 0:main],
                                                  whi[:, b, 0:main].bitcast(F32), ALU.subtract)
                if up:
                    c = slice(main or BCOL, (main or BCOL) + P)
                    ins = up_rows(whi[:, b, c], raw[:, s, c])
                if before:
                    ins = factor_lo(whi[:, b, DCOL:SPL].rearrange("p (b c) -> p b c", b=NB),
                                    raw[:, s, DCOL:RAW].rearrange("p (b r) -> p b r", b=NB), SCALE1)
                if last:
                    ins.then_inc(split_done[s], 1)

            def rows_lo(at, n):
                dve.wait_ge(h_ready[n], at(1, 1))
                for j in range(NB):
                    p, c = slice(GRP * j, GRP * (j + 1)), slice(BATCH * j, BATCH * (j + 1))
                    ins = nc.vector.scalar_tensor_tensor(t_rows[n][p, c], t_copy[n][p, c], mask_sb[p, 0:1],
                                                         t_bank[n][p, c], ALU.mult, ALU.add)
                ins.then_inc(r_done[n], 1)

            def x_lo(at, src, layer, k):
                dve.wait_ge(a_hi, at(N_A, layer * KH + k + 1))
                nc.vector.tensor_tensor(xlo[:, k, :], src[:, k, :], xhi[:, k, :].bitcast(F32),
                                        ALU.subtract).then_inc(a_done, 1)

            def product(at, f, i=0):
                dve.wait_ge(silu_done, at(FT, f + 1) + i * 2)
                if f == FT - 1:
                    nc.vector.tensor_tensor(acc[2][0:TAIL, :], scratch[0:TAIL, :], acc[2][TAIL:P, :],
                                            ALU.mult).then_inc(prod_done, 1)
                else:
                    w = wnum(I_GU + 2 * f + 1)
                    dve.wait_ge(slot_done[1], at(PC_SPLIT[1], w // 2 + 1) + i * 2)
                    up = acc[2 * (f % 2) + 1][:]
                    nc.vector.tensor_tensor(up, scratch[:], up, ALU.mult).then_inc(prod_done, 1)

            def hidden_lo(at, f, i=0):
                dve.wait_ge(act_hi, at(FT, f + 1) + i * 2)
                if f < FULL:
                    k = slice(f, f + 1) if isinstance(i, int) else bass.ds(i * 2 + f, 1)
                    lo = actlo[:, k, :].rearrange("p o n -> p (o n)")
                    hi = acthi[:, k, :].rearrange("p o n -> p (o n)")
                    nc.vector.tensor_tensor(lo, acc[2 * (f % 2) + 1][:], hi.bitcast(F32),
                                            ALU.subtract).then_inc(act_done, 1)
                else:
                    nc.vector.tensor_tensor(tail[TAIL:P, :], acc[2][0:TAIL, :], tail[0:TAIL, :].bitcast(F32),
                                            ALU.subtract).then_inc(act_done, 1)

            def a0_lo(at):
                dve.wait_ge(hi_done, at(NPIECE, I_A0 + 1))
                for j in range(NB):
                    ins = factor_lo(ax0[:, :, GRP * j:GRP * (j + 1)],
                                    raw[:, I_A0, P * j:P * (j + 1)].rearrange("p (k r) -> p k r", r=RANK), SCALE0)
                ins.then_inc(split_done[I_A0], 1)

            def last_layers(at, h):
                if 0 <= h + 1 < KH:
                    s = h + 1
                    dve.wait_ge(x3_sum, at(KH, s + 1))
                    y = res2[:, s, :]
                    nc.vector.tensor_tensor(y, x3_bank[s % 2][:], y, ALU.add).then_inc(x3_done, 1)
                if h == V_ROWS:
                    rows_lo(at, T3)
                if 0 <= h - FIRST_X4 < KH // 2:
                    for m in (2 * (h - FIRST_X4), 2 * (h - FIRST_X4) + 1):
                        dve.wait_ge(x4_sum, at(KH, m + 1))
                        y = res2[:, m, :]
                        nc.vector.tensor_tensor(y, x4_bank[m % 3][:], y, ALU.add).then_inc(x4_done, 1)

            def x1_chunk(at, m):
                dve.wait_ge(slot_done[m % 2], at(PC_SPLIT[m % 2], m // 2 + 1))
                y = res[:, m, :]
                nc.vector.scalar_tensor_tensor(y, acc[m % 4][:], bias_sb[:, m:m + 1], y,
                                               ALU.add, ALU.add).then_inc(x1_done, 1)

            def head(at, prev=None):
                for k in range(KH):
                    x_lo(at, res, 0, k)
                    if k == FIRST_K - 1:
                        split_lo(at, I_L0)
                    if prev and k == 5:
                        rows_lo(prev, T2)
                split_lo(at, I_L0 + 1)
                rows_lo(at, T0)
                if prev:
                    last_layers(prev, -1)
                for m in range(KH):
                    if m and prev:
                        last_layers(prev, 2 * m - 2)
                        last_layers(prev, 2 * m - 1)
                    if m < KH - 1:
                        x1_chunk(at, m)
                    if m == KH - 2:
                        dve.wait_ge(hi_done, at(NPIECE, I_AG + 1))
                        pair_lo(I_AG % RAWS, SCALE1).then_inc(split_done[I_AG % RAWS], 1)
                        split_lo(at, I_GU)
                    elif m < KH - 2:
                        split_lo(at, I_L0 + m + 2)

            def mid(at, more):
                for k in range(KH):
                    if k == KH - 1:
                        x1_chunk(at, k)
                    x_lo(at, res, 1, k)
                split_lo(at, I_GU + 1)
                rows_lo(at, TG)
                rows_lo(at, TU)
                with dve.Fori(0, (FT - 2) // 2) as i:
                    for f in range(2):
                        split_lo(at, I_GU + 2 * (f + 1), i, RAWS)
                        product(at, f, i)
                        split_lo(at, I_GU + 2 * (f + 1) + 1, i, RAWS, before=True)
                        hidden_lo(at, f, i)
                f = FT - 2
                split_lo(at, I_GU + 2 * (f + 1))
                product(at, f)
                split_lo(at, I_LAST_UP, main=0, before=True, last=False)
                s = I_LAST_UP % RAWS
                pair_lo(s, 1.0)
                factor_lo(ax0[:, 0, :].rearrange("p (b c) -> p b c", b=NB),
                          raw[:, s, UVCOL:UVCOL + NB * RANK].rearrange("p (b r) -> p b r", b=NB),
                          SCALE1).then_inc(split_done[s], 1)
                split_lo(at, I_DN, up=False)
                hidden_lo(at, f)
                split_lo(at, I_DN + 1, up=False)
                product(at, FT - 1)
                hidden_lo(at, FT - 1)
                dve.wait_ge(out_done, at(16 * KH, 16))
                for d in range(3 * KH):
                    m = d // 3
                    if d % 3 == 2:
                        w = wnum(I_DN + d)
                        dve.wait_ge(slot_done[w % 2], at(PC_SPLIT[w % 2], w // 2 + 1))
                        nc.vector.tensor_tensor(res2[:, m, :], acc[m % 4][:], res[:, m, :], ALU.add).then_inc(x2_done, 1)
                        x_lo(at, res2, 2, m)
                    if d + 2 < 3 * KH:
                        q = (d + 2) % 3
                        split_lo(at, I_DN + d + 2, main=DN_TILES[q] * P, up=q == 2)
                    if d == 0:
                        rows_lo(at, TD)
                    if d == 3 * KH - 3:
                        for k in (I_S2, I_S3):
                            dve.wait_ge(hi_done, at(NPIECE, k + 1))
                            up_rows(bx[:, k - I_S2, :], raw[:, k % RAWS, 0:BCOL]).then_inc(split_done[k % RAWS], 1)
                    if more and d == 3 * KH - 3:
                        a0_lo(At(at.t, at.off + 1))

            for n, r in enumerate((r0, r1, r2)):
                nc.vector.memset(r[:].bitcast(F32), 0.0).then_inc(zeroed, 1)
            dve.wait_ge(zeroed, 3)
            dve.sem_inc(prod_done, 1)
            dve.wait_ge(const_in, 32)
            a0_lo(At(0))
            head(At(0))
            with dve.Fori(0, NTB - 1) as t:
                mid(At(t), True)
                head(At(t, 1), At(t))
            at = At(NTB - 1)
            mid(at, False)
            rows_lo(at, T2)
            for h in range(-1, FIRST_X4 + KH // 2):
                last_layers(at, h)

        @block.tensor
        def _(pe):
            def mm(dst, stationary, moving, start, stop):
                return pe.matmul(dst, stationary, moving, start=start, stop=stop)

            def wait_piece(at, idx, i=0, per_step=0):
                s = idx % RAWS
                pe.wait_ge(split_done[s], at(PC_RAW, idx // RAWS + 1) + i * (per_step // RAWS))

            def thrice(dst, b, j, hi, lo, start):
                c = slice(j * P, (j + 1) * P)
                mm(dst, whi[:, b, c], hi, start, False)
                mm(dst, whi[:, b, c], lo, False, False)
                return mm(dst, wlo[:, b, c], hi, False, False)

            def width(dst, b, chunks=range(KH), last=False):
                for k in chunks:
                    ins = thrice(dst, b, k, xhi[:, k, :], xlo[:, k, :], k == 0)
                    if last:
                        ins.then_inc(x_used, 1)

            def factor_chunk(at, layer, n, factor, k):
                pe.wait_ge(a_done, at(N_A, layer * KH + k + 1))
                mm(t_bank[n][:], factor[:, k, :], xhi[:, k, :], k == 0, False)
                ins = mm(t_bank[n][:], factor[:, k, :], xlo[:, k, :], False, k == KH - 1)
                if n == T2:
                    ins.then_inc(x_used, 1)
                elif k == KH - 1:
                    ins.then_inc(t_full[n], 1)

            def hidden_down(at, f, stationary, i=0):
                pe.wait_ge(act_done, at(FT, f + 1) + i * 2)
                if f < FULL:
                    k = slice(f, f + 1) if isinstance(i, int) else bass.ds(i * 2 + f, 1)
                    mm(t_bank[TD][:], stationary, acthi[:, k, :].rearrange("p o n -> p (o n)"), f == 0, False)
                    return mm(t_bank[TD][:], stationary, actlo[:, k, :].rearrange("p o n -> p (o n)"), False, False)
                return mm(t_bank[TD][:], stationary, tail[:], False, True)

            def gate_up(at, h, i, f0, first=False, before=True):
                f = f0 + h
                g = I_GU + 2 * f
                gate, up = acc[2 * (f % 2)][:], acc[2 * (f % 2) + 1][:]
                if first:
                    pe.wait_ge(x1_done, at(KH, 6 + 2 * h))
                else:
                    pe.wait_ge(act_done, at(FT, f - 1) + i * 2)
                wait_piece(at, g, i, RAWS)
                width(gate, 0)
                if f == 0:
                    pe.wait_ge(r_done[TG], at(1, 1))
                mm(gate, whi[:, 0, BCOL:DCOL], r1[:], False, f < FT - 1).then_inc(slot_done[0], 1)
                wait_piece(at, g + 1, i, RAWS)
                if f == 0:
                    width(up, 1)
                    pe.wait_ge(r_done[TU], at(1, 1))
                    ins = mm(up, whi[:, 1, BCOL:DCOL], r2[:], False, True)
                elif f < FT - 1:
                    width(up, 1)
                    ins = mm(up, whi[:, 1, BCOL:DCOL], r2[:], False, True)
                else:
                    mm(gate, whi[:, 1, BCOL:DCOL], r2[:], False, True).then_inc(last_up_done, 1)
                if before:
                    ins = hidden_down(at, f - 1, whi[:, 1, DCOL:SPL], i)
                if f < FT - 1:
                    ins.then_inc(slot_done[1], 1)

            def last_layers(at, h):
                if 0 <= h + 1 < KH:
                    s = h + 1
                    if s == 0:
                        pe.wait_ge(r_done[T2], at(1, 1))
                    if s >= 2:
                        pe.wait_ge(x3_done, at(KH, s - 1))
                    mm(x3_bank[s % 2][:], bx[:, 0, s * P:(s + 1) * P], r1[:], True, True).then_inc(x3_sum, 1)
                if 0 <= h - 1 < KH:
                    k = h - 1
                    pe.wait_ge(x3_split, at(KH, k + 1))
                    mm(t_bank[T3][:], axp[:, 1, k, :], x3hi[:, k % 2, :], k == 0, False)
                    mm(t_bank[T3][:], axp[:, 1, k, :], x3lo[:, k % 2, :], False, k == KH - 1
                       ).then_inc(x3_used if k < KH - 1 else t_full[T3], 1)
                if 0 <= h - FIRST_X4 < KH // 2:
                    for m in (2 * (h - FIRST_X4), 2 * (h - FIRST_X4) + 1):
                        if m == 0:
                            pe.wait_ge(r_done[T3], at(1, 1))
                            pe.wait_ge(x3_done, at(KH, KH))
                        if m >= 3:
                            pe.wait_ge(x4_done, at(KH, m - 2))
                        mm(x4_bank[m % 3][:], bx[:, 1, m * P:(m + 1) * P], r2[:], True, True).then_inc(x4_sum, 1)

            def head(at, prev=None):
                wait_piece(at, I_A0)
                first = [(k, n) for k in range(KH) for n in range(3)]

                def first_mm():
                    k, n = first.pop(0)
                    c = slice(k * P, (k + 1) * P)
                    mm(acc[0][:], (wlo if n == 2 else whi)[:, 0, c], (xlo if n == 1 else xhi)[:, k, :],
                       k == 0 and n == 0, False)

                for k in range(KH):
                    factor_chunk(at, 0, T0, ax0, k)
                    if k == FIRST_K:
                        wait_piece(at, I_L0)
                    if k >= FIRST_K:
                        first_mm()
                if prev:
                    last_layers(prev, -1)
                while first:
                    first_mm()
                for m in range(KH):
                    if m >= 4:
                        pe.wait_ge(x1_done, at(KH, m - 3))
                    if m:
                        wait_piece(at, I_L0 + m)
                        for half in range(2):
                            if prev:
                                last_layers(prev, 2 * (m - 1) + half)
                            width(acc[m % 4][:], m % 2, range(4 * half, 4 * half + 4), m == KH - 1)
                    else:
                        pe.wait_ge(r_done[T0], at(1, 1))
                    mm(acc[m % 4][:], whi[:, m % 2, BCOL:DCOL], r0[:], False, True).then_inc(slot_done[m % 2], 1)
                if prev:
                    pe.wait_ge(x4_done, prev(KH, KH))

            def mid(at):
                wait_piece(at, I_AG)
                for k in range(KH):
                    factor_chunk(at, 1, TG, axp[:, 0], k)
                    factor_chunk(at, 1, TU, axp[:, 1], k)
                gate_up(at, 0, 0, 0, first=True, before=False)
                gate_up(at, 1, 0, 0, first=True)
                with pe.Fori(0, (FT - 4) // 2) as i:
                    for h in range(2):
                        gate_up(at, h, i, 2)
                gate_up(at, 0, 0, FT - 2)
                gate_up(at, 1, 0, FT - 2)
                for m in range(KH):
                    dst = acc[m % 4][:]
                    if m >= 4:
                        pe.wait_ge(x2_done, at(KH, m - 3))
                    else:
                        pe.wait_ge(act_done, at(FT, FT - 1 + m // 2))
                    for q, tiles in enumerate(DN_TILES):
                        k = I_DN + 3 * m + q
                        b = wnum(k) % 2
                        wait_piece(at, k)
                        for j in range(tiles):
                            f = sum(DN_TILES[:q]) + j
                            if f < FULL:
                                ins = thrice(dst, b, j, acthi[:, f, :], actlo[:, f, :], f == 0)
                            else:
                                mm(dst, whi[:, b, j * P:(j + 1) * P], tail[:], False, False)
                                mm(dst, wlo[:, b, j * P:(j + 1) * P], tail[:], False, False)
                        if q == 2:
                            if m == 0:
                                pe.wait_ge(r_done[TD], at(1, 1))
                            ins = mm(dst, whi[:, b, tiles * P:(tiles + 1) * P], r0[:], False, True)
                        ins.then_inc(slot_done[b], 1)
                        if m == 0 and q == 0:
                            hidden_down(at, FT - 1, ax0[:, 0, :]).then_inc(t_full[TD], 1)
                for k in range(KH):
                    factor_chunk(at, 2, T2, axp[:, 0], k)

            head(At(0))
            with pe.Fori(0, NTB - 1) as t:
                mid(At(t))
                head(At(t, 1), At(t))
            at = At(NTB - 1)
            mid(at)
            for h in range(-1, FIRST_X4 + KH // 2):
                last_layers(at, h)


def kernel(**inputs):
    import concourse.bacc as bacc
    from concourse.bass_utils import run_bass_kernel_spmd

    a = {k: np.ascontiguousarray(v) for k, v in inputs.items()}

    def chunks(w):
        n, k, m = w.shape
        return w.reshape(n, k // P, P, m).transpose(0, 2, 1, 3).reshape(n, P, k // P * m)

    def four(w):
        return np.concatenate([w] * 4, axis=1)

    def tiles(w):
        n, r, c = w.shape
        return w.reshape(n, r, c // P, P).transpose(0, 2, 1, 3)

    x = a["x"].reshape(NTB, TB, KH, P).transpose(0, 2, 3, 1)
    w0 = chunks(a["L0_cond_W"].reshape(KH, P, H).transpose(0, 2, 1))
    gate, up = a["L1_cond_W_gate"], a["L1_cond_W_up"]
    gu = np.stack([gate[:FULL * P].reshape(FULL, P, H), up[:FULL * P].reshape(FULL, P, H)], axis=1)
    gu = gu.reshape(2 * FULL, P, H)
    gu = np.concatenate([gu, np.concatenate([gate[FULL * P:], up[FULL * P:]])[None]])
    wgu = chunks(gu.transpose(0, 2, 1))
    dt = a["L1_cond_W_down"].T
    dt = np.concatenate([dt, dt[FULL * P:]])
    wdn = chunks(dt.reshape(FT * P, KH, P).transpose(1, 0, 2))
    a0 = chunks(a["L0_cond_lora_As"])
    agu = np.concatenate([chunks(a["L1_cond_A_gate"][0].transpose(0, 2, 1)),
                          chunks(a["L1_cond_A_up"][0].transpose(0, 2, 1))], axis=2)
    b0 = tiles(four(a["L0_cond_lora_Bs"]))
    bgt = a["L1_cond_B_gate"][0].transpose(0, 2, 1)
    but = a["L1_cond_B_up"][0].transpose(0, 2, 1)
    zero = np.zeros_like(bgt[:, :, :TAIL])
    bg = tiles(four(np.concatenate([bgt, zero], axis=2)))
    bu = tiles(four(np.concatenate([but[:, :, :FULL * P], zero, but[:, :, FULL * P:]], axis=2)))
    adt = a["L1_cond_A_down"][0].transpose(0, 2, 1)
    adt = np.concatenate([adt, adt[:, FULL * P:]], axis=1)
    ad = adt.reshape(adt.shape[0], FT, P, RANK)
    bd = tiles(four(a["L1_cond_B_down"][0].transpose(0, 2, 1)))
    uf = chunks(a["L2_cond_B"].transpose(0, 2, 1))
    vf = chunks(a["L3_cond_B"].transpose(0, 2, 1))
    s2 = four(a["L2_cond_A"].transpose(0, 2, 1))
    s3 = four(a["L3_cond_A"].transpose(0, 2, 1))
    bias = a["L0_cond_b"].reshape(KH, P).T
    ids = np.stack([a[n].reshape(NTB, NB) for n in ("itok_B_0_23", "itok_B_2_6", "itok_B_4_50", "itok_B_3_7")], axis=1)
    ids = ids.reshape(1, NTB * 4 * NB)
    masks = np.zeros((P, 2), np.float32)
    masks[np.arange(P) // RANK % 4 == 1, 0] = -1.0
    masks[np.arange(P) // RANK % 4 == 2, 1] = -1.0

    names = ("x", "bias", "idx", "w0", "wgu", "wdn", "a0", "agu", "b0", "bg", "bu", "ad", "bd", "uf", "vf", "s2", "s3",
             "masks")
    given = (x, bias, ids, w0, wgu, wdn, a0, agu, b0, bg, bu, ad, bd, uf, vf, s2, s3, masks)
    nc = bacc.Bacc("TRN2", target_bir_lowering=False, num_devices=1,
                   dynamic_dma_scratch_size=1024)
    arrays, args = {}, []
    for name, v in zip(names, given):
        v = np.ascontiguousarray(v)
        arrays[f"in_{name}"] = v
        args.append(nc.dram_tensor(f"in_{name}", v.shape, mybir.dt.from_np(v.dtype), kind="ExternalInput").ap())
    out = nc.dram_tensor("out_y", (NTB, KH, P, TB), F32, kind="ExternalOutput").ap()
    adapted_layers(nc, *args, out)
    got = run_bass_kernel_spmd(nc, [arrays], core_ids=[0]).results[0]["out_y"]
    return got.transpose(0, 3, 1, 2).reshape(TOKENS // BATCH, BATCH, H)
```

```python
from contextlib import ExitStack

import numpy as np

import concourse.bass as bass
from concourse import mybir

ALU = mybir.AluOpType
ACT = mybir.ActivationFunctionType
F32 = mybir.dt.float32
F32R = mybir.dt.float32r
I32 = mybir.dt.int32

P = 128
TOKENS, H, F, RANK = 2048, 1024, 2752, 16
BATCH = 256
TB = 512
NTB = TOKENS // TB
NB = TB // BATCH
KH = H // P
FULL = F // P
FT = FULL + 1
TAIL = F - FULL * P
GRP = 4 * RANK
SCALE0, SCALE1 = 2.0, 0.5

I_A0 = 0
I_L0 = 1
I_AG = I_L0 + KH
I_GU = I_AG + 1
I_LAST_UP = I_GU + 2 * FT - 1
I_DN = I_GU + 2 * FT
I_S2 = I_DN + 3 * KH
I_S3 = I_S2 + 1
NPIECE = I_S3 + 1
RAWS = 4
assert NPIECE % RAWS == 0 and TAIL * 2 == P

BCOL = KH * P
DCOL = BCOL + P
RAW = DCOL + NB * RANK
SPL = DCOL + P
UVCOL = 2 * P * NB
A2COL = UVCOL + NB * RANK
DN_TILES = (8, 8, 6)

LOADS = [0] * NPIECE
LOADS[I_A0] = LOADS[I_AG] = NB
for _m in range(KH):
    LOADS[I_L0 + _m] = 1 + NB
for _f in range(FT):
    LOADS[I_GU + 2 * _f] = 1 + NB
    LOADS[I_GU + 2 * _f + 1] = 1 + NB + (NB if _f else 0)
LOADS[I_LAST_UP] = 6 * NB
for _m in range(KH):
    LOADS[I_DN + 3 * _m] = LOADS[I_DN + 3 * _m + 1] = 1
    LOADS[I_DN + 3 * _m + 2] = 1 + NB
LOADS[I_S2] = LOADS[I_S3] = NB
SLOT_LOADS = [sum(LOADS[s::RAWS]) for s in range(RAWS)]


def landed(idx):
    return sum(LOADS[idx % RAWS:idx + 1:RAWS])


def wnum(idx):
    return idx - 1 if idx < I_AG else idx - 2 if idx <= I_LAST_UP else idx - 3


NW = wnum(I_S2)

PC_RAW = NPIECE // RAWS
PC_SPLIT = ((NW + 1) // 2, NW // 2)
N_A = 3 * KH


class At:
    def __init__(self, t, off=0):
        self.t, self.off = t, off

    def __call__(self, per_block, n):
        return self.t * per_block + (self.off * per_block + n)


FIRST_OUT = 3
FOLD_AT = (3, 6)
UV_AT = 4
HALVES = [slice(h * BCOL // 2, (h + 1) * BCOL // 2) for h in range(2)]
FIRST_K = 4

PICK_HI0, PICK_LO0, PICK_HI1, PICK_LO1, SUM1, V_HI, V_LO, NPICK = range(8)


def adapted_layers(nc, x, bias, idx, w0, wgu, wdn, a0, agu, b0, bg, bu, ad, bd, uf, vf, a2, s2, s3, masks,
                   picks, out):
    with ExitStack() as ctx:
        def sb(name, shape, dt):
            return ctx.enter_context(nc.sbuf_tensor(name, shape, dt))

        def sem(name):
            return ctx.enter_context(nc.semaphore(name))

        xhi = sb("xhi", [P, KH, TB], F32R)
        xlo = sb("xlo", [P, KH, TB], F32R)
        acthi = sb("acthi", [P, FULL, TB], F32R)
        actlo = sb("actlo", [P, FULL, TB], F32R)
        tail = sb("tail", [P, TB], F32R)
        res = sb("res", [P, KH, TB], F32)
        res2 = sb("res2", [P, KH, TB], F32)
        ax0 = sb("ax0", [P, KH, P], F32R)
        axp = sb("axp", [P, KH, P], F32R)
        ga = sb("ga", [P, KH, 2 * NB * RANK], F32R)
        fold_hi = sb("fold_hi", [P, P], F32R)
        fold_lo = sb("fold_lo", [P, P], F32R)
        pick = sb("pick", [P, NPICK, P], F32R)
        bx = sb("bx", [P, 2, BCOL], F32R)
        r0 = sb("r0", [P, TB], F32R)
        r1 = sb("r1", [P, TB], F32R)
        r2 = sb("r2", [P, TB], F32R)
        scratch = sb("scratch", [P, TB], F32)
        whi = sb("whi", [P, 2, SPL], F32R)
        wlo = sb("wlo", [P, 2, BCOL], F32R)
        raw = sb("raw", [P, RAWS, RAW], F32)
        bias_sb = sb("bias_sb", [P, KH], F32)
        mask_sb = sb("mask_sb", [P, 2], F32)
        idx_sb = sb("idx_sb", [1, NTB * 4 * NB], I32)
        acc = [ctx.enter_context(nc.psum_tensor(f"acc{i}", [P, TB], F32)) for i in range(4)]
        tps = [ctx.enter_context(nc.psum_tensor(f"tps{i}", [P, TB], F32)) for i in range(4)]
        T0, TD, TV = range(3)
        t_bank = [tps[0], tps[3], tps[3]]
        t_rows = [r0, r0, r2]
        GU, UV = range(2)
        pair_bank = [tps[0], tps[1]]
        pick_bank = [(tps[1], tps[2]), (tps[2], tps[3])]
        fold_bank = [tps[1], tps[2]]
        x4_bank = [tps[1], tps[2], tps[3]]

        idx_in = sem("idx_in")
        bias_in = sem("bias_in")
        masks_in = sem("masks_in")
        picks_landed = sem("picks_landed")
        zeroed = sem("zeroed")
        x_full = [sem(f"x_full{k}") for k in range(KH)]
        raw_full = [sem(f"raw_full{s}") for s in range(RAWS)]
        first_in = [sem(f"first_in{h}") for h in range(2)]
        first_hi = sem("first_hi")
        first_split = sem("first_split")
        hi_done = sem("hi_done")
        split_done = [sem(f"split_done{s}") for s in range(RAWS)]
        slot_done = [sem(f"slot_done{s}") for s in range(2)]
        pick_done = sem("pick_done")
        last_up_done = sem("last_up_done")
        t_full = [sem(f"t_full{n}") for n in range(3)]
        h_ready = [sem(f"h_ready{n}") for n in range(3)]
        r_done = [sem(f"r_done{n}") for n in range(3)]
        gu_full = sem("gu_full")
        pair_hi_done = [sem(f"pair_hi_done{n}") for n in range(2)]
        pair_split = [sem(f"pair_split{n}") for n in range(2)]
        picked = [sem(f"picked{n}") for n in range(2)]
        rows_ready = [sem(f"rows_ready{n}") for n in range(2)]
        fold_sum = sem("fold_sum")
        fold_rounded = sem("fold_rounded")
        fold_split = sem("fold_split")
        x_used = sem("x_used")
        a_hi = sem("a_hi")
        a_done = sem("a_done")
        x1_done = sem("x1_done")
        x2_done = sem("x2_done")
        x4_done = sem("x4_done")
        x4_sum = sem("x4_sum")
        silu_done = sem("silu_done")
        prod_done = sem("prod_done")
        act_hi = sem("act_hi")
        act_done = sem("act_done")
        out_done = sem("out_done")

        picks_in = res2[:, 0:2, :].rearrange("p f n -> p (f n)")[:, 0:NPICK * P]

        block = ctx.enter_context(nc.Block())

        def of_batch(tile, j):
            return tile[GRP * j:GRP * (j + 1), BATCH * j:BATCH * (j + 1)]

        def pair_cols(tile, j, part):
            return tile[:, :, GRP * j:GRP * (j + 1)].rearrange("p k (t q) -> p t k q", t=2)[
                :, :, :, RANK * part:RANK * (part + 1)]

        def pair_raw(s, j):
            return raw[:, s, 2 * P * j:2 * P * (j + 1)].rearrange("p (t k r) -> p t k r", t=2, k=KH)

        def a2_cols(part):
            return ga[:].rearrange("p k (b q) -> p b k q", b=NB)[:, :, :, RANK * part:RANK * (part + 1)]

        def a2_raw(s):
            return raw[:, s, A2COL:A2COL + P * NB].rearrange("p (b k r) -> p b k r", b=NB, k=KH)

        def fold_src():
            return fold_bank[0][:, 0:NB * RANK].rearrange("p (b r) -> p b r", b=NB).unsqueeze(2).to_broadcast(
                [P, NB, 4, RANK])

        @block.sync
        def _(sp):
            def load_piece(at, idx0, step, per_step, parts):
                s = idx0 % RAWS
                n = at(PC_RAW, idx0 // RAWS)
                if not (isinstance(n, int) and n == 0):
                    sp.wait_ge(split_done[s], n + step * (per_step // RAWS))
                for dst, src in parts:
                    sp.dma_start(dst(s), src).then_inc(raw_full[s], 16)

            def cols(a, b):
                return lambda s: raw[:, s, a:b]

            def rows(j, a, b):
                return lambda s: raw[GRP * j:GRP * (j + 1), s, a:b]

            def of(array, i):
                return array[bass.ds(i, 1)].rearrange("o p c -> (o p) c")

            def of2(array, i, k):
                return array[bass.ds(i, 1), bass.ds(k, 1)].rearrange("o q p c -> (o q p) c")

            def adapter(t, kind, top):
                return [sp.value_load(idx_sb[0:1, bass.ds(t * (4 * NB) + (NB * kind + j), 1)],
                                      min_val=0, max_val=top.shape[0] - 1) for j in range(NB)]

            def a0_piece(at, e0):
                load_piece(at, I_A0, 0, 0, [(cols(P * j, P * (j + 1)), of(a0, e0[j])) for j in range(NB)])

            def l0_piece(at, i, m, e0, weights=True):
                load_piece(at, I_L0 + m, i, RAWS,
                           ([(cols(0, BCOL), of(w0, i * RAWS + m))] if weights else [])
                           + [(rows(j, BCOL, DCOL), of2(b0, e0[j], i * RAWS + m)) for j in range(NB)])

            def gate_up(at, i, f0, e1, before=(True, True)):
                for h in range(2):
                    f = i * 2 + (f0 + h)
                    g = i * 4 + 2 * (f0 + h)
                    k = I_GU + 2 * (f0 + h)
                    load_piece(at, k, i, RAWS,
                               [(cols(0, BCOL), of(wgu, g))]
                               + [(rows(j, BCOL, DCOL), of2(bg, e1[j], f)) for j in range(NB)])
                    if k + 1 < I_LAST_UP:
                        load_piece(at, k + 1, i, RAWS,
                                   [(cols(0, BCOL), of(wgu, g + 1))]
                                   + [(rows(j, BCOL, DCOL), of2(bu, e1[j], f)) for j in range(NB)]
                                   + ([(cols(DCOL + RANK * j, DCOL + RANK * (j + 1)), of2(ad, e1[j], f - 1))
                                       for j in range(NB)] if before[h] else []))

            def mid(t, at):
                e1, e2, e3 = adapter(t, 1, agu), adapter(t, 2, uf), adapter(t, 3, vf)
                load_piece(at, I_AG, 0, 0, [(cols(2 * P * j, 2 * P * (j + 1)), of(agu, e1[j])) for j in range(NB)])
                gate_up(at, 0, 0, e1, (False, True))
                with sp.Fori(0, (FT - 4) // 2) as i:
                    gate_up(at, i, 2, e1)
                gate_up(at, 0, FT - 2, e1)
                load_piece(at, I_LAST_UP, 0, 0,
                           [(rows(j, BCOL, DCOL), of2(bu, e1[j], FT - 1)) for j in range(NB)]
                           + [(cols(DCOL + RANK * j, DCOL + RANK * (j + 1)), of2(ad, e1[j], FT - 2)) for j in range(NB)]
                           + [(cols(2 * P * j, 2 * P * j + P), of(uf, e2[j])) for j in range(NB)]
                           + [(cols(2 * P * j + P, 2 * P * j + 2 * P), of(vf, e3[j])) for j in range(NB)]
                           + [(cols(UVCOL + RANK * j, UVCOL + RANK * (j + 1)), of2(ad, e1[j], FT - 1))
                              for j in range(NB)]
                           + [(cols(A2COL + P * j, A2COL + P * (j + 1)), of(a2, e2[j])) for j in range(NB)])
                with sp.Fori(0, 2) as i:
                    for m in range(4):
                        for q in range(3):
                            w = DN_TILES[q] * P
                            c = sum(DN_TILES[:q]) * P
                            load_piece(at, I_DN + 3 * m + q, i, 3 * 4,
                                       [(cols(0, w), of(wdn, i * 4 + m)[:, c:c + w])]
                                       + ([(rows(j, w, w + P), of2(bd, e1[j], i * 4 + m)) for j in range(NB)]
                                          if q == 2 else []))
                load_piece(at, I_S2, 0, 0, [(rows(j, 0, BCOL), of(s2, e2[j])) for j in range(NB)])
                load_piece(at, I_S3, 0, 0, [(rows(j, 0, BCOL), of(s3, e3[j])) for j in range(NB)])

            sp.dma_start(idx_sb[:], idx).then_inc(idx_in, 16)
            for h in range(2):
                sp.dma_start(raw[:, I_L0, HALVES[h]], w0[0][:, HALVES[h]]).then_inc(first_in[h], 16)
                sp.dma_start(res[:, h, :], x[0, h]).then_inc(x_full[h], 16)
            sp.wait_ge(idx_in, 16)
            at = At(0)
            e0 = adapter(0, 0, a0)
            sp.dma_start(res[:, 2, :], x[0, 2]).then_inc(x_full[2], 16)
            a0_piece(at, e0)
            for k in range(3, KH):
                sp.dma_start(res[:, k, :], x[0, k]).then_inc(x_full[k], 16)
                if k == 4:
                    sp.dma_start(mask_sb[:], masks).then_inc(masks_in, 16)
                    l0_piece(at, 0, 0, e0, weights=False)
            sp.dma_start(bias_sb[:], bias).then_inc(bias_in, 16)
            for m in range(1, KH):
                l0_piece(at, 0, m, e0)
                if m == 2:
                    sp.dma_start(picks_in, picks).then_inc(picks_landed, 16)
            with sp.Fori(0, NTB - 1) as t:
                mid(t, At(t))
                e0 = adapter(t + 1, 0, a0)
                a0_piece(At(t, 1), e0)
                with sp.Fori(0, KH // RAWS) as i:
                    for m in range(RAWS):
                        l0_piece(At(t, 1), i, m, e0)
            mid(NTB - 1, At(NTB - 1))

        @block.scalar
        def _(act):
            def rounded(dst, src, scale=1.0):
                return nc.scalar.activation(dst, src, ACT.Copy, scale=scale)

            def diagonal(dst, src):
                for j in range(NB):
                    ins = rounded(of_batch(dst, j), of_batch(src, j))
                return ins

            def factor_hi(dst, src, scale):
                n = src.shape[1]
                return rounded(dst[:, :, 0:3 * RANK].rearrange("p n (g r) -> p n g r", g=3),
                               src.unsqueeze(2).to_broadcast([P, n, 3, RANK]), scale)

            def pair_hi(s, scale):
                for j in range(NB):
                    ins = rounded(pair_cols(axp, j, 0), pair_raw(s, j), scale)
                return ins

            def wait_raw(at, idx, i=0, per_step=0):
                s = idx % RAWS
                step = landed(idx + per_step) - landed(idx)
                act.wait_ge(raw_full[s], at(16 * SLOT_LOADS[s], 16 * landed(idx)) + i * (16 * step))

            def split_hi(at, idx, i=0, per_step=0, main=BCOL, up=True, before=False, last=True):
                s, w = idx % RAWS, wnum(idx)
                wait_raw(at, idx, i, per_step)
                n = at(PC_SPLIT[w % 2], w // 2)
                if not (isinstance(n, int) and n == 0):
                    act.wait_ge(slot_done[w % 2], n + i * (per_step // 2))
                lo, hi = (0 if main else BCOL), (main or BCOL) + (P if up else 0)
                ins = rounded(whi[:, w % 2, lo:hi], raw[:, s, lo:hi])
                if before:
                    ins = factor_hi(whi[:, w % 2, DCOL:SPL].rearrange("p (b c) -> p b c", b=NB),
                                    raw[:, s, DCOL:RAW].rearrange("p (b r) -> p b r", b=NB), SCALE1)
                if last:
                    ins.then_inc(hi_done, 1)

            def rows_hi(at, n, sem_before, value):
                act.wait_ge(t_full[n], at(1, 1))
                if sem_before is not None:
                    act.wait_ge(sem_before, value)
                diagonal(scratch[:].bitcast(F32R), t_bank[n]).then_inc(h_ready[n], 1)

            def pair_rows_hi(at, n):
                if n == UV:
                    act.wait_ge(x_used, at(2 * KH, 2 * KH))
                else:
                    act.wait_ge(gu_full, at(1, 1))
                diagonal(r1, pair_bank[n]).then_inc(pair_hi_done[n], 1)

            def fold(at, h):
                act.wait_ge(fold_sum, at(2, h + 1))
                if h == 0:
                    rounded(fold_hi[:].rearrange("p (b g r) -> p b g r", b=NB, g=4), fold_src()
                            ).then_inc(fold_rounded, 1)
                else:
                    for j in range(NB):
                        p = slice(GRP * j, GRP * j + GRP // 2)
                        ins = rounded(pick[p, V_HI, :], fold_bank[1][p, 0:P])
                    ins.then_inc(fold_rounded, 1)

            def x_hi(src, k):
                rounded(xhi[:, k, :], src[:, k, :]).then_inc(a_hi, 1)

            def silu(at, f, i=0):
                w = wnum(I_GU + 2 * f)
                if f == FT - 1:
                    act.wait_ge(last_up_done, at(1, 1))
                    p = slice(0, TAIL)
                else:
                    act.wait_ge(slot_done[0], at(PC_SPLIT[0], w // 2 + 1) + i * 2)
                    p = slice(0, P)
                act.wait_ge(prod_done, at(FT, f + 1) + i * 2)
                nc.scalar.activation(scratch[p, :], acc[2 * (f % 2)][p, :], ACT.Silu).then_inc(silu_done, 1)

            def hidden_hi(at, f, i=0):
                act.wait_ge(prod_done, at(FT, f + 2) + i * 2)
                if f < FULL:
                    k = slice(f, f + 1) if isinstance(i, int) else bass.ds(i * 2 + f, 1)
                    rounded(acthi[:, k, :].rearrange("p o n -> p (o n)"), acc[2 * (f % 2) + 1][:]).then_inc(act_hi, 1)
                else:
                    rounded(tail[0:TAIL, :], acc[2][0:TAIL, :]).then_inc(act_hi, 1)

            def a0_hi(at):
                wait_raw(at, I_A0)
                for j in range(NB):
                    ins = factor_hi(ax0[:, :, GRP * j:GRP * (j + 1)],
                                    raw[:, I_A0, P * j:P * (j + 1)].rearrange("p (k r) -> p k r", r=RANK), SCALE0)
                ins.then_inc(hi_done, 1)

            def last_rows(at, sem_before, value):
                rows_hi(at, TV, sem_before, value)
                act.wait_ge(picked[UV], at(1, 1))
                diagonal(r1, pick_bank[UV][0]).then_inc(rows_ready[UV], 1)

            def store(t, at, h):
                m = h - FIRST_OUT - 1
                if 0 <= m < KH:
                    act.wait_ge(x4_done, at(KH, m + 1))
                    act.dma_start(out[bass.ds(t, 1), m].rearrange("o p c -> (o p) c"), res2[:, m, :]
                                  ).then_inc(out_done, 16)

            def start(at):
                for k in range(KH):
                    if k < 2:
                        act.wait_ge(first_in[k], 16)
                        rounded(whi[:, 0, HALVES[k]], raw[:, I_L0, HALVES[k]]).then_inc(first_hi, 1)
                    act.wait_ge(x_full[k], 16)
                    x_hi(res, k)
                    if k == 1:
                        act.sem_inc(raw_full[I_L0], 16)
                    if k == FIRST_K - 1:
                        a0_hi(at)
                split_hi(at, I_L0, main=0)

            def head(at, prev=None):
                if not prev:
                    start(at)
                for k in range(KH if prev else 0):
                    act.wait_ge(x_full[k], at(16, 16))
                    act.wait_ge(x_used, prev[1](2 * KH, KH + k + 1))
                    x_hi(res, k)
                    if k == UV_AT:
                        pair_rows_hi(prev[1], UV)
                split_hi(at, I_L0 + 1)
                if prev:
                    rows_hi(at, T0, r_done[TD], prev[1](1, 1))
                else:
                    rows_hi(at, T0, None, 0)
                for m in range(KH):
                    if m == 1 and prev:
                        last_rows(prev[1], r_done[T0], at(1, 1))
                    if m and prev:
                        store(*prev, 2 * m - 2)
                        store(*prev, 2 * m - 1)
                    if m == KH - 2:
                        wait_raw(at, I_AG)
                        act.wait_ge(slot_done[1], at(PC_SPLIT[1], 3))
                        pair_hi(I_AG % RAWS, SCALE1).then_inc(hi_done, 1)
                        split_hi(at, I_GU)
                    elif m < KH - 2:
                        split_hi(at, I_L0 + m + 2)

            def mid(t, at, more):
                for k in range(KH):
                    act.wait_ge(x1_done, at(KH, k + 1))
                    act.wait_ge(x_used, at(2 * KH, k + 1))
                    x_hi(res, k)
                split_hi(at, I_GU + 1)
                pair_rows_hi(at, GU)
                act.wait_ge(picked[GU], at(1, 1))
                diagonal(r1, pick_bank[GU][0]).then_inc(rows_ready[GU], 1)
                diagonal(r2, pick_bank[GU][1]).then_inc(rows_ready[GU], 1)
                with act.Fori(0, (FT - 2) // 2) as i:
                    for f in range(2):
                        split_hi(at, I_GU + 2 * (f + 1), i, RAWS)
                        silu(at, f, i)
                        split_hi(at, I_GU + 2 * (f + 1) + 1, i, RAWS, before=True)
                        hidden_hi(at, f, i)
                f = FT - 2
                split_hi(at, I_GU + 2 * (f + 1))
                silu(at, f)
                split_hi(at, I_LAST_UP, main=0, before=True, last=False)
                act.wait_ge(gu_full, at(1, 1))
                s = I_LAST_UP % RAWS
                pair_hi(s, 1.0)
                rounded(a2_cols(0), a2_raw(s))
                factor_hi(ax0[:, 0, :].rearrange("p (b c) -> p b c", b=NB),
                          raw[:, s, UVCOL:UVCOL + NB * RANK].rearrange("p (b r) -> p b r", b=NB),
                          SCALE1).then_inc(hi_done, 1)
                split_hi(at, I_DN, up=False)
                hidden_hi(at, f)
                split_hi(at, I_DN + 1, up=False)
                silu(at, FT - 1)
                hidden_hi(at, FT - 1)
                for d in range(3 * KH):
                    m = d // 3
                    if more and d == 3 * KH - 1:
                        split_hi(At(at.t, at.off + 1), I_L0)
                    if d % 3 == 2:
                        act.wait_ge(x2_done, at(KH, m + 1))
                        x_hi(res2, m)
                        if more:
                            act.dma_start(res[:, m, :], x[bass.ds(t + 1, 1), m].rearrange("o p c -> (o p) c")
                                          ).then_inc(x_full[m], 16)
                    if d + 2 < 3 * KH:
                        q = (d + 2) % 3
                        split_hi(at, I_DN + d + 2, main=DN_TILES[q] * P, up=q == 2)
                    if d == 0:
                        rows_hi(at, TD, prod_done, at(FT, FT + 1))
                    if d in FOLD_AT:
                        fold(at, FOLD_AT.index(d))
                    if d == 3 * KH - 3:
                        for k in (I_S2, I_S3):
                            wait_raw(at, k)
                            rounded(bx[:, k - I_S2, :], raw[:, k % RAWS, 0:BCOL]).then_inc(hi_done, 1)
                    if more and d == 3 * KH - 3:
                        a0_hi(At(at.t, at.off + 1))

            act.sem_inc(out_done, 16)
            act.wait_ge(zeroed, 1)
            nc.scalar.activation(scratch[:, 0:1], r0[:, 0:1].bitcast(F32), ACT.Silu)
            head(At(0))
            act.wait_ge(picks_landed, 16)
            rounded(pick[:].rearrange("p n c -> p (n c)"), picks_in).then_inc(pick_done, 1)
            with act.Fori(0, NTB - 1) as t:
                mid(t, At(t), True)
                head(At(t, 1), (t, At(t)))
            t, at = NTB - 1, At(NTB - 1)
            mid(t, at, False)
            pair_rows_hi(at, UV)
            last_rows(at, r_done[TD], at(1, 1))
            for m in range(KH):
                store(t, at, m + FIRST_OUT + 1)
            act.wait_ge(out_done, 16 + 16 * KH * NTB)

        @block.vector
        def _(dve):
            def factor_lo(dst, src, scale):
                return nc.vector.scalar_tensor_tensor(dst[:, :, 3 * RANK:GRP], src, scale,
                                                      dst[:, :, 0:RANK].bitcast(F32), ALU.mult, ALU.subtract)

            def pair_lo(s, scale):
                for j in range(NB):
                    for t in range(2):
                        ins = nc.vector.scalar_tensor_tensor(
                            pair_cols(axp, j, 1)[:, t], pair_raw(s, j)[:, t], scale,
                            pair_cols(axp, j, 0)[:, t].bitcast(F32), ALU.mult, ALU.subtract)
                return ins

            def up_rows(dst, src):
                return nc.vector.scalar_tensor_tensor(dst, dst.bitcast(F32), mask_sb[:, 1:2], src, ALU.mult, ALU.add)

            def split_lo(at, idx, i=0, per_step=0, main=BCOL, up=True, before=False, last=True):
                s, b = idx % RAWS, wnum(idx) % 2
                dve.wait_ge(hi_done, at(NPIECE, idx + 1) + i * per_step)
                if main:
                    ins = nc.vector.tensor_tensor(wlo[:, b, 0:main], raw[:, s, 0:main],
                                                  whi[:, b, 0:main].bitcast(F32), ALU.subtract)
                if up:
                    c = slice(main or BCOL, (main or BCOL) + P)
                    ins = up_rows(whi[:, b, c], raw[:, s, c])
                if before:
                    ins = factor_lo(whi[:, b, DCOL:SPL].rearrange("p (b c) -> p b c", b=NB),
                                    raw[:, s, DCOL:RAW].rearrange("p (b r) -> p b r", b=NB), SCALE1)
                if last:
                    ins.then_inc(split_done[s], 1)

            def rows_lo(at, n):
                dve.wait_ge(h_ready[n], at(1, 1))
                if n == TV:
                    dve.wait_ge(picked[UV], at(1, 1))
                for j in range(NB):
                    ins = nc.vector.scalar_tensor_tensor(of_batch(t_rows[n], j), of_batch(scratch, j),
                                                         mask_sb[GRP * j:GRP * (j + 1), 0:1],
                                                         of_batch(t_bank[n], j), ALU.mult, ALU.add)
                ins.then_inc(r_done[n], 1)

            def pair_rows_lo(at, n):
                dve.wait_ge(pair_hi_done[n], at(1, 1))
                for j in range(NB):
                    ins = nc.vector.tensor_tensor(of_batch(r2, j), of_batch(pair_bank[n], j),
                                                  of_batch(r1, j).bitcast(F32), ALU.subtract)
                ins.then_inc(pair_split[n], 1)

            def fold(at, h):
                dve.wait_ge(fold_rounded, at(2, h + 1))
                if h == 0:
                    def four(tile):
                        return tile[:].rearrange("p (b g r) -> p b g r", b=NB, g=4)
                    nc.vector.tensor_tensor(four(fold_lo), fold_src(), four(fold_hi).bitcast(F32), ALU.subtract
                                            ).then_inc(fold_split, 1)
                else:
                    for j in range(NB):
                        p = slice(GRP * j, GRP * j + GRP // 2)
                        ins = nc.vector.tensor_tensor(pick[p, V_LO, :], fold_bank[1][p, 0:P],
                                                      pick[p, V_HI, :].bitcast(F32), ALU.subtract)
                    ins.then_inc(fold_split, 1)

            def x_lo(at, src, layer, k):
                dve.wait_ge(a_hi, at(N_A, layer * KH + k + 1))
                nc.vector.tensor_tensor(xlo[:, k, :], src[:, k, :], xhi[:, k, :].bitcast(F32),
                                        ALU.subtract).then_inc(a_done, 1)

            def product(at, f, i=0):
                dve.wait_ge(silu_done, at(FT, f + 1) + i * 2)
                if f == FT - 1:
                    nc.vector.tensor_tensor(acc[2][0:TAIL, :], scratch[0:TAIL, :], acc[2][TAIL:P, :],
                                            ALU.mult).then_inc(prod_done, 1)
                else:
                    w = wnum(I_GU + 2 * f + 1)
                    dve.wait_ge(slot_done[1], at(PC_SPLIT[1], w // 2 + 1) + i * 2)
                    up = acc[2 * (f % 2) + 1][:]
                    nc.vector.tensor_tensor(up, scratch[:], up, ALU.mult).then_inc(prod_done, 1)

            def hidden_lo(at, f, i=0):
                dve.wait_ge(act_hi, at(FT, f + 1) + i * 2)
                if f < FULL:
                    k = slice(f, f + 1) if isinstance(i, int) else bass.ds(i * 2 + f, 1)
                    lo = actlo[:, k, :].rearrange("p o n -> p (o n)")
                    hi = acthi[:, k, :].rearrange("p o n -> p (o n)")
                    nc.vector.tensor_tensor(lo, acc[2 * (f % 2) + 1][:], hi.bitcast(F32),
                                            ALU.subtract).then_inc(act_done, 1)
                else:
                    nc.vector.tensor_tensor(tail[TAIL:P, :], acc[2][0:TAIL, :], tail[0:TAIL, :].bitcast(F32),
                                            ALU.subtract).then_inc(act_done, 1)

            def a0_lo(at):
                dve.wait_ge(hi_done, at(NPIECE, I_A0 + 1))
                for j in range(NB):
                    ins = factor_lo(ax0[:, :, GRP * j:GRP * (j + 1)],
                                    raw[:, I_A0, P * j:P * (j + 1)].rearrange("p (k r) -> p k r", r=RANK), SCALE0)
                ins.then_inc(split_done[I_A0], 1)

            def x4_chunk(at, h):
                m = h - FIRST_OUT
                if 0 <= m < KH:
                    dve.wait_ge(x4_sum, at(KH, m + 1))
                    y = res2[:, m, :]
                    nc.vector.tensor_tensor(y, x4_bank[m % 3][:], y, ALU.add).then_inc(x4_done, 1)

            def x1_chunk(at, m):
                dve.wait_ge(slot_done[m % 2], at(PC_SPLIT[m % 2], m // 2 + 1))
                y = res[:, m, :]
                nc.vector.scalar_tensor_tensor(y, acc[m % 4][:], bias_sb[:, m:m + 1], y,
                                               ALU.add, ALU.add).then_inc(x1_done, 1)

            def start(at):
                for k in range(KH):
                    if k < 2:
                        dve.wait_ge(first_hi, k + 1)
                        nc.vector.tensor_tensor(wlo[:, 0, HALVES[k]], raw[:, I_L0, HALVES[k]],
                                                whi[:, 0, HALVES[k]].bitcast(F32), ALU.subtract
                                                ).then_inc(first_split, 1)
                    x_lo(at, res, 0, k)
                    if k == FIRST_K - 1:
                        a0_lo(at)
                dve.wait_ge(masks_in, 16)
                split_lo(at, I_L0, main=0)

            def head(at, prev=None):
                if not prev:
                    start(at)
                for k in range(KH if prev else 0):
                    x_lo(at, res, 0, k)
                    if k == UV_AT:
                        pair_rows_lo(prev, UV)
                split_lo(at, I_L0 + 1)
                rows_lo(at, T0)
                if not prev:
                    dve.wait_ge(bias_in, 16)
                for m in range(KH):
                    if m == 1 and prev:
                        rows_lo(prev, TV)
                    if m and prev:
                        x4_chunk(prev, 2 * m - 2)
                        x4_chunk(prev, 2 * m - 1)
                    if m < KH - 1:
                        x1_chunk(at, m)
                    if m == KH - 2:
                        dve.wait_ge(hi_done, at(NPIECE, I_AG + 1))
                        pair_lo(I_AG % RAWS, SCALE1).then_inc(split_done[I_AG % RAWS], 1)
                        split_lo(at, I_GU)
                    elif m < KH - 2:
                        split_lo(at, I_L0 + m + 2)

            def mid(at, more):
                for k in range(KH):
                    if k == KH - 1:
                        x1_chunk(at, k)
                    x_lo(at, res, 1, k)
                split_lo(at, I_GU + 1)
                pair_rows_lo(at, GU)
                with dve.Fori(0, (FT - 2) // 2) as i:
                    for f in range(2):
                        split_lo(at, I_GU + 2 * (f + 1), i, RAWS)
                        product(at, f, i)
                        split_lo(at, I_GU + 2 * (f + 1) + 1, i, RAWS, before=True)
                        hidden_lo(at, f, i)
                f = FT - 2
                split_lo(at, I_GU + 2 * (f + 1))
                product(at, f)
                split_lo(at, I_LAST_UP, main=0, before=True, last=False)
                s = I_LAST_UP % RAWS
                pair_lo(s, 1.0)
                nc.vector.tensor_tensor(a2_cols(1), a2_raw(s), a2_cols(0).bitcast(F32), ALU.subtract)
                factor_lo(ax0[:, 0, :].rearrange("p (b c) -> p b c", b=NB),
                          raw[:, s, UVCOL:UVCOL + NB * RANK].rearrange("p (b r) -> p b r", b=NB),
                          SCALE1).then_inc(split_done[s], 1)
                split_lo(at, I_DN, up=False)
                hidden_lo(at, f)
                split_lo(at, I_DN + 1, up=False)
                product(at, FT - 1)
                hidden_lo(at, FT - 1)
                dve.wait_ge(out_done, at(16 * KH, 16))
                for d in range(3 * KH):
                    m = d // 3
                    if d % 3 == 2:
                        w = wnum(I_DN + d)
                        dve.wait_ge(slot_done[w % 2], at(PC_SPLIT[w % 2], w // 2 + 1))
                        nc.vector.tensor_tensor(res2[:, m, :], acc[m % 4][:], res[:, m, :], ALU.add).then_inc(x2_done, 1)
                        if more and m == KH - 1:
                            split_lo(At(at.t, at.off + 1), I_L0)
                        x_lo(at, res2, 2, m)
                    if d + 2 < 3 * KH:
                        q = (d + 2) % 3
                        split_lo(at, I_DN + d + 2, main=DN_TILES[q] * P, up=q == 2)
                    if d == 0:
                        rows_lo(at, TD)
                    if d in FOLD_AT:
                        fold(at, FOLD_AT.index(d))
                    if d == 3 * KH - 3:
                        for k in (I_S2, I_S3):
                            dve.wait_ge(hi_done, at(NPIECE, k + 1))
                            up_rows(bx[:, k - I_S2, :], raw[:, k % RAWS, 0:BCOL]).then_inc(split_done[k % RAWS], 1)
                    if more and d == 3 * KH - 3:
                        a0_lo(At(at.t, at.off + 1))

            for n, r in enumerate((r0, r1, r2)):
                nc.vector.memset(r[:].bitcast(F32), 0.0).then_inc(zeroed, 1)
            dve.wait_ge(zeroed, 3)
            dve.sem_inc(prod_done, 1)
            head(At(0))
            with dve.Fori(0, NTB - 1) as t:
                mid(At(t), True)
                head(At(t, 1), At(t))
            at = At(NTB - 1)
            mid(at, False)
            pair_rows_lo(at, UV)
            rows_lo(at, TV)
            for m in range(KH):
                x4_chunk(at, m + FIRST_OUT)

        @block.tensor
        def _(pe):
            def mm(dst, stationary, moving, start, stop):
                return pe.matmul(dst, stationary, moving, start=start, stop=stop)

            def wait_piece(at, idx, i=0, per_step=0):
                s = idx % RAWS
                pe.wait_ge(split_done[s], at(PC_RAW, idx // RAWS + 1) + i * (per_step // RAWS))

            def thrice(dst, b, j, hi, lo, start):
                c = slice(j * P, (j + 1) * P)
                mm(dst, whi[:, b, c], hi, start, False)
                mm(dst, whi[:, b, c], lo, False, False)
                return mm(dst, wlo[:, b, c], hi, False, False)

            def width(dst, b, chunks=range(KH), last=False):
                for k in chunks:
                    ins = thrice(dst, b, k, xhi[:, k, :], xlo[:, k, :], k == 0)
                    if last:
                        ins.then_inc(x_used, 1)

            def factor_chunk(at, layer, bank, factor, k):
                pe.wait_ge(a_done, at(N_A, layer * KH + k + 1))
                mm(bank[:], factor[:, k, :], xhi[:, k, :], k == 0, False)
                return mm(bank[:], factor[:, k, :], xlo[:, k, :], False, k == KH - 1)

            def pick_rows(at, n):
                pe.wait_ge(pair_split[n], at(1, 1))
                a, b = pick_bank[n]
                if n == UV:
                    pe.wait_ge(fold_split, at(2, 2))
                    mm(b[:], pick[:, V_HI, :], r1[:], True, False)
                    mm(b[:], pick[:, V_HI, :], r2[:], False, False)
                    mm(b[:], pick[:, V_LO, :], r1[:], False, True).then_inc(t_full[TV], 1)
                mm(a[:], pick[:, PICK_HI0, :], r1[:], True, False)
                ins = mm(a[:], pick[:, PICK_LO0, :], r2[:], False, True)
                if n == GU:
                    mm(b[:], pick[:, PICK_HI1, :], r1[:], True, False)
                    ins = mm(b[:], pick[:, PICK_LO1, :], r2[:], False, True)
                ins.then_inc(picked[n], 1)

            def fold(at, h):
                if h == 0:
                    dst = fold_bank[0][:, 0:NB * RANK]
                    for k in range(KH):
                        for part in range(2):
                            ins = mm(dst, axp[:, k, :], ga[:, k, :].rearrange("p (b q) -> p b q", b=NB)[
                                :, :, RANK * part:RANK * (part + 1)], k == 0 and part == 0, k == KH - 1 and part == 1)
                else:
                    dst = fold_bank[1][:, 0:P]
                    pe.wait_ge(fold_split, at(2, 1))
                    mm(dst, fold_hi[:], pick[:, SUM1, :], True, False)
                    ins = mm(dst, fold_lo[:], pick[:, SUM1, :], False, True)
                ins.then_inc(fold_sum, 1)

            def hidden_down(at, f, stationary, i=0):
                pe.wait_ge(act_done, at(FT, f + 1) + i * 2)
                if f < FULL:
                    k = slice(f, f + 1) if isinstance(i, int) else bass.ds(i * 2 + f, 1)
                    mm(t_bank[TD][:], stationary, acthi[:, k, :].rearrange("p o n -> p (o n)"), f == 0, False)
                    return mm(t_bank[TD][:], stationary, actlo[:, k, :].rearrange("p o n -> p (o n)"), False, False)
                return mm(t_bank[TD][:], stationary, tail[:], False, True)

            def first_gate_up(at):
                gate, up = acc[0][:], acc[1][:]
                pe.wait_ge(x1_done, at(KH, 6))
                wait_piece(at, I_AG)
                todo = [(k, n) for k in range(KH) for n in range(3)]

                def gate_mm():
                    k, n = todo.pop(0)
                    mm(gate, (wlo if n == 2 else whi)[:, 0, k * P:(k + 1) * P], (xlo if n == 1 else xhi)[:, k, :],
                       k == 0 and n == 0, False)

                for k in range(KH):
                    ins = factor_chunk(at, 1, pair_bank[GU], axp, k)
                    if k == KH - 1:
                        ins.then_inc(gu_full, 1)
                    if k == 0:
                        wait_piece(at, I_GU)
                    gate_mm()
                    gate_mm()
                while todo:
                    gate_mm()
                pick_rows(at, GU)
                wait_piece(at, I_GU + 1)
                width(up, 1, range(0, 3))
                pe.wait_ge(rows_ready[GU], at(2, 1))
                mm(gate, whi[:, 0, BCOL:DCOL], r1[:], False, True).then_inc(slot_done[0], 1)
                width(up, 1, range(3, KH))
                pe.wait_ge(rows_ready[GU], at(2, 2))
                mm(up, whi[:, 1, BCOL:DCOL], r2[:], False, True).then_inc(slot_done[1], 1)

            def gate_up(at, h, i, f0, first=False, before=True):
                f = f0 + h
                g = I_GU + 2 * f
                gate, up = acc[2 * (f % 2)][:], acc[2 * (f % 2) + 1][:]
                if first:
                    pe.wait_ge(x1_done, at(KH, KH))
                else:
                    pe.wait_ge(act_done, at(FT, f - 1) + i * 2)
                wait_piece(at, g, i, RAWS)
                width(gate, 0)
                mm(gate, whi[:, 0, BCOL:DCOL], r1[:], False, f < FT - 1).then_inc(slot_done[0], 1)
                wait_piece(at, g + 1, i, RAWS)
                if f < FT - 1:
                    width(up, 1)
                    ins = mm(up, whi[:, 1, BCOL:DCOL], r2[:], False, True)
                else:
                    mm(gate, whi[:, 1, BCOL:DCOL], r2[:], False, True).then_inc(last_up_done, 1)
                if before:
                    ins = hidden_down(at, f - 1, whi[:, 1, DCOL:SPL], i)
                if f < FT - 1:
                    ins.then_inc(slot_done[1], 1)

            def x4_chunk(at, h):
                m = h - FIRST_OUT
                if not 0 <= m < KH:
                    return
                if m == 0:
                    pe.wait_ge(rows_ready[UV], at(1, 1))
                    pe.wait_ge(r_done[TV], at(1, 1))
                if m >= 3:
                    pe.wait_ge(x4_done, at(KH, m - 2))
                mm(x4_bank[m % 3][:], bx[:, 0, m * P:(m + 1) * P], r1[:], True, False)
                mm(x4_bank[m % 3][:], bx[:, 1, m * P:(m + 1) * P], r2[:], False, True).then_inc(x4_sum, 1)

            def head(at, prev=None):
                first = [(k, n) for k in range(KH) for n in range(3)]

                def first_mm():
                    k, n = first.pop(0)
                    c = slice(k * P, (k + 1) * P)
                    mm(acc[0][:], (wlo if n == 2 else whi)[:, 0, c], (xlo if n == 1 else xhi)[:, k, :],
                       k == 0 and n == 0, False)

                if prev:
                    wait_piece(at, I_L0)
                else:
                    for k in range(FIRST_K):
                        pe.wait_ge(first_split, k // 2 + 1)
                        pe.wait_ge(a_done, k + 1)
                        for _ in range(3):
                            first_mm()
                    pe.wait_ge(first_split, 2)
                wait_piece(at, I_A0)
                for k in range(KH):
                    ins = factor_chunk(at, 0, t_bank[T0], ax0, k)
                    if k == KH - 1:
                        ins.then_inc(t_full[T0], 1)
                    for _ in range(2 if prev else k // FIRST_K):
                        first_mm()
                if prev:
                    pick_rows(prev, UV)
                while first:
                    first_mm()
                for m in range(KH):
                    if m >= 4:
                        pe.wait_ge(x1_done, at(KH, m - 3))
                    if m:
                        wait_piece(at, I_L0 + m)
                        for half in range(2):
                            if prev:
                                x4_chunk(prev, 2 * (m - 1) + half)
                            width(acc[m % 4][:], m % 2, range(4 * half, 4 * half + 4), m == KH - 1)
                    else:
                        if not prev:
                            wait_piece(at, I_L0)
                        pe.wait_ge(r_done[T0], at(1, 1))
                    mm(acc[m % 4][:], whi[:, m % 2, BCOL:DCOL], r0[:], False, True).then_inc(slot_done[m % 2], 1)
                if prev:
                    pe.wait_ge(x4_done, prev(KH, KH))

            def mid(at):
                first_gate_up(at)
                gate_up(at, 1, 0, 0, first=True)
                with pe.Fori(0, (FT - 4) // 2) as i:
                    for h in range(2):
                        gate_up(at, h, i, 2)
                gate_up(at, 0, 0, FT - 2)
                gate_up(at, 1, 0, FT - 2)
                for m in range(KH):
                    dst = acc[m % 4][:]
                    if m >= 4:
                        pe.wait_ge(x2_done, at(KH, m - 3))
                    else:
                        pe.wait_ge(act_done, at(FT, FT - 1 + m // 2))
                    for q, tiles in enumerate(DN_TILES):
                        k = I_DN + 3 * m + q
                        b = wnum(k) % 2
                        if 3 * m + q in FOLD_AT:
                            fold(at, FOLD_AT.index(3 * m + q))
                        wait_piece(at, k)
                        for j in range(tiles):
                            f = sum(DN_TILES[:q]) + j
                            if f < FULL:
                                ins = thrice(dst, b, j, acthi[:, f, :], actlo[:, f, :], f == 0)
                            else:
                                mm(dst, whi[:, b, j * P:(j + 1) * P], tail[:], False, False)
                                mm(dst, wlo[:, b, j * P:(j + 1) * P], tail[:], False, False)
                        if q == 2:
                            if m == 0:
                                pe.wait_ge(r_done[TD], at(1, 1))
                            ins = mm(dst, whi[:, b, tiles * P:(tiles + 1) * P], r0[:], False, True)
                        ins.then_inc(slot_done[b], 1)
                        if m == 0 and q == 0:
                            hidden_down(at, FT - 1, ax0[:, 0, :]).then_inc(t_full[TD], 1)
                for k in range(KH):
                    factor_chunk(at, 2, pair_bank[UV], axp, k).then_inc(x_used, 1)

            head(At(0))
            pe.wait_ge(pick_done, 1)
            with pe.Fori(0, NTB - 1) as t:
                mid(At(t))
                head(At(t, 1), At(t))
            at = At(NTB - 1)
            mid(at)
            pick_rows(at, UV)
            for m in range(KH):
                x4_chunk(at, m + FIRST_OUT)


def kernel(**inputs):
    import concourse.bacc as bacc
    from concourse.bass_utils import run_bass_kernel_spmd

    a = {k: np.ascontiguousarray(v) for k, v in inputs.items()}

    def chunks(w):
        n, k, m = w.shape
        return w.reshape(n, k // P, P, m).transpose(0, 2, 1, 3).reshape(n, P, k // P * m)

    def four(w):
        return np.concatenate([w] * 4, axis=1)

    def tiles(w):
        n, r, c = w.shape
        return w.reshape(n, r, c // P, P).transpose(0, 2, 1, 3)

    x = a["x"].reshape(NTB, TB, KH, P).transpose(0, 2, 3, 1)
    w0 = chunks(a["L0_cond_W"].reshape(KH, P, H).transpose(0, 2, 1))
    gate, up = a["L1_cond_W_gate"], a["L1_cond_W_up"]
    gu = np.stack([gate[:FULL * P].reshape(FULL, P, H), up[:FULL * P].reshape(FULL, P, H)], axis=1)
    gu = gu.reshape(2 * FULL, P, H)
    gu = np.concatenate([gu, np.concatenate([gate[FULL * P:], up[FULL * P:]])[None]])
    wgu = chunks(gu.transpose(0, 2, 1))
    dt = a["L1_cond_W_down"].T
    dt = np.concatenate([dt, dt[FULL * P:]])
    wdn = chunks(dt.reshape(FT * P, KH, P).transpose(1, 0, 2))
    a0 = chunks(a["L0_cond_lora_As"])
    agu = np.concatenate([chunks(a["L1_cond_A_gate"][0].transpose(0, 2, 1)),
                          chunks(a["L1_cond_A_up"][0].transpose(0, 2, 1))], axis=2)
    b0 = tiles(four(a["L0_cond_lora_Bs"]))
    bgt = a["L1_cond_B_gate"][0].transpose(0, 2, 1)
    but = a["L1_cond_B_up"][0].transpose(0, 2, 1)
    zero = np.zeros_like(bgt[:, :, :TAIL])
    bg = tiles(four(np.concatenate([bgt, zero], axis=2)))
    bu = tiles(four(np.concatenate([but[:, :, :FULL * P], zero, but[:, :, FULL * P:]], axis=2)))
    adt = a["L1_cond_A_down"][0].transpose(0, 2, 1)
    adt = np.concatenate([adt, adt[:, FULL * P:]], axis=1)
    ad = adt.reshape(adt.shape[0], FT, P, RANK)
    bd = tiles(four(a["L1_cond_B_down"][0].transpose(0, 2, 1)))
    uf = chunks(a["L2_cond_B"].transpose(0, 2, 1))
    vf = chunks(a["L3_cond_B"].transpose(0, 2, 1))
    a2 = chunks(a["L2_cond_A"])
    s2 = four(a["L2_cond_A"].transpose(0, 2, 1))
    s3 = four(a["L3_cond_A"].transpose(0, 2, 1))
    bias = a["L0_cond_b"].reshape(KH, P).T
    ids = np.stack([a[n].reshape(NTB, NB) for n in ("itok_B_0_23", "itok_B_2_6", "itok_B_4_50", "itok_B_3_7")], axis=1)
    ids = ids.reshape(1, NTB * 4 * NB)
    masks = np.zeros((P, 2), np.float32)
    masks[np.arange(P) // RANK % 4 == 1, 0] = -1.0
    masks[np.arange(P) // RANK % 4 == 2, 1] = -1.0

    picks = np.zeros((P, NPICK, P), np.float32)
    for j in range(NB):
        for r in range(RANK):
            for n, src, dst in ((PICK_HI0, 0, (0, 2)), (PICK_HI0, 1, (3,)), (PICK_LO0, 0, (1,)),
                                (PICK_HI1, 2, (0, 2)), (PICK_HI1, 3, (3,)), (PICK_LO1, 2, (1,)),
                                (SUM1, 2, (0, 1, 2)), (SUM1, 3, (0, 1, 2)), (V_HI, 2, (0, 1, 2)), (V_HI, 3, (0, 1, 2))):
                for g in dst:
                    picks[GRP * j + RANK * src + r, n, GRP * j + RANK * g + r] = 1.0
    picks = picks.reshape(P, NPICK * P)

    names = ("x", "bias", "idx", "w0", "wgu", "wdn", "a0", "agu", "b0", "bg", "bu", "ad", "bd", "uf", "vf", "a2", "s2",
             "s3", "masks", "picks")
    given = (x, bias, ids, w0, wgu, wdn, a0, agu, b0, bg, bu, ad, bd, uf, vf, a2, s2, s3, masks, picks)
    nc = bacc.Bacc("TRN2", target_bir_lowering=False, num_devices=1,
                   dynamic_dma_scratch_size=1024)
    arrays, args = {}, []
    for name, v in zip(names, given):
        v = np.ascontiguousarray(v)
        arrays[f"in_{name}"] = v
        args.append(nc.dram_tensor(f"in_{name}", v.shape, mybir.dt.from_np(v.dtype), kind="ExternalInput").ap())
    out = nc.dram_tensor("out_y", (NTB, KH, P, TB), F32, kind="ExternalOutput").ap()
    adapted_layers(nc, *args, out)
    got = run_bass_kernel_spmd(nc, [arrays], core_ids=[0]).results[0]["out_y"]
    return got.transpose(0, 3, 1, 2).reshape(TOKENS // BATCH, BATCH, H)
```
